# Optimizing a Trainium2 kernel written in Bass

```python
import numpy as np
import jax
import jax.numpy as jnp

def _softmax(x, axis=-1):
    return jax.nn.softmax(x, axis=axis)

def _gelu(x):
    return jax.nn.gelu(x, approximate=True)

def _silu(x):
    return jax.nn.silu(x)

def _sigmoid(x):
    return jax.nn.sigmoid(x)

def _layernorm(x, axis=-1, eps=1e-05):
    m = jnp.mean(x, axis=axis, keepdims=True)
    v = jnp.var(x, axis=axis, keepdims=True)
    return (x - m) / jnp.sqrt(v + eps)

def _scatter_add(tgt, idx, src, axis=0):
    return tgt.at[idx].add(src)

def _segment_sum(src, seg, n):
    return jax.ops.segment_sum(src, seg, n)
kernel_name = 'mk_gnn_resnorm_d1_gnn_r64_6111ef'

def setup_inputs(seed: int=0):
    np.random.seed(seed)
    _w = jnp.asarray

    def _rec_inputs():
        import jax
        import jax.numpy as jnp
        _gk = jax.random.key(seed)
        x = -0.000202 + 1 * jax.random.normal(jax.random.fold_in(_gk, 1), (100000, 128), jnp.float32)
        src = jax.random.randint(jax.random.fold_in(_gk, 2), (25000,), 0, 100000, jnp.int32)
        dst = jnp.minimum((100000 * jax.random.uniform(jax.random.fold_in(_gk, 3), (25000,)) ** 2.0).astype(jnp.int32), 99999)
        _o = jnp.argsort(dst, stable=True)
        src = src[_o]
        dst = dst[_o]
        edge_attr_64 = jax.random.uniform(jax.random.fold_in(_gk, 12), (25000, 64), jnp.float32, 0.0, 1)
        return (x, src, dst, edge_attr_64)
    x, src, dst, edge_attr_64 = _rec_inputs()

    def _L0_gnn_setup():
        import jax, jax.numpy as jnp
        import numpy as np
        LN2 = 0.6931471805599453

        def ssp(x):
            return jax.nn.softplus(x) - LN2
        N_ATOMS, N_EDGES, K_RBF, F_DIM, N_RES = (50000, 10000, 64, 128, 3)
        key = jax.random.key(seed)
        ks = jax.random.split(key, 16)
        sF = 1.0 / np.sqrt(F_DIM)
        sK = 1.0 / np.sqrt(K_RBF)
        return {'x': jax.random.normal(ks[0], (N_ATOMS, F_DIM), jnp.float32), 'rbf': jax.random.uniform(ks[1], (N_EDGES, K_RBF), jnp.float32), 'idx_i': jnp.sort(jax.random.randint(ks[2], (N_EDGES,), 0, N_ATOMS, jnp.int64)), 'idx_j': jax.random.randint(ks[3], (N_EDGES,), 0, N_ATOMS, jnp.int64), 'W_k2f': jax.random.normal(ks[4], (K_RBF, F_DIM), jnp.float32) * sK, 'W_i': jax.random.normal(ks[5], (F_DIM, F_DIM), jnp.float32) * sF, 'b_i': jnp.zeros((F_DIM,), jnp.float32), 'W_j': jax.random.normal(ks[6], (F_DIM, F_DIM), jnp.float32) * sF, 'b_j': jnp.zeros((F_DIM,), jnp.float32), 'W_res1': jax.random.normal(ks[7], (N_RES, F_DIM, F_DIM), jnp.float32) * sF, 'b_res1': jnp.zeros((N_RES, F_DIM), jnp.float32), 'W_res2': jax.random.normal(ks[8], (N_RES, F_DIM, F_DIM), jnp.float32) * sF, 'b_res2': jnp.zeros((N_RES, F_DIM), jnp.float32), 'W_out': jax.random.normal(ks[9], (F_DIM, F_DIM), jnp.float32) * sF, 'b_out': jnp.zeros((F_DIM,), jnp.float32), 'u': jnp.ones((F_DIM,), jnp.float32)}
    _L0_gnn_all = _L0_gnn_setup()
    _L0_gnn_in = {k: v for k, v in _L0_gnn_all.items() if k in ('W_k2f', 'W_i', 'b_i', 'W_j', 'b_j', 'W_res1', 'b_res1', 'W_res2', 'b_res2', 'W_out', 'b_out', 'u')}
    del _L0_gnn_all
    return {'x': x, 'src': src, 'dst': dst, 'edge_attr_64': edge_attr_64, 'L0_gnn_W_k2f': _L0_gnn_in['W_k2f'], 'L0_gnn_W_i': _L0_gnn_in['W_i'], 'L0_gnn_b_i': _L0_gnn_in['b_i'], 'L0_gnn_W_j': _L0_gnn_in['W_j'], 'L0_gnn_b_j': _L0_gnn_in['b_j'], 'L0_gnn_W_res1': _L0_gnn_in['W_res1'], 'L0_gnn_b_res1': _L0_gnn_in['b_res1'], 'L0_gnn_W_res2': _L0_gnn_in['W_res2'], 'L0_gnn_b_res2': _L0_gnn_in['b_res2'], 'L0_gnn_W_out': _L0_gnn_in['W_out'], 'L0_gnn_b_out': _L0_gnn_in['b_out'], 'L0_gnn_u': _L0_gnn_in['u']}

def reference(x, src, dst, edge_attr_64, L0_gnn_W_k2f, L0_gnn_W_i, L0_gnn_b_i, L0_gnn_W_j, L0_gnn_b_j, L0_gnn_W_res1, L0_gnn_b_res1, L0_gnn_W_res2, L0_gnn_b_res2, L0_gnn_W_out, L0_gnn_b_out, L0_gnn_u):
    import jax
    import jax.numpy as jnp

    def _L0_gnn_ref(x, rbf, idx_i, idx_j, W_k2f, W_i, b_i, W_j, b_j, W_res1, b_res1, W_res2, b_res2, W_out, b_out, u):
        import jax, jax.numpy as jnp
        import numpy as np
        LN2 = 0.6931471805599453

        def ssp(x):
            return jax.nn.softplus(x) - LN2
        N_ATOMS, N_EDGES, K_RBF, F_DIM, N_RES = (50000, 10000, 64, 128, 3)
        n_atoms = x.shape[0]
        xa = ssp(x)
        g = rbf @ W_k2f
        xi = ssp(xa @ W_i + b_i)
        xj_feat = ssp(xa @ W_j + b_j)
        pxj = g * xj_feat[idx_j]
        xj = jax.ops.segment_sum(pxj, idx_i, num_segments=n_atoms)
        m = xi + xj
        for l in range(W_res1.shape[0]):
            y = ssp(m)
            m = m + (ssp(y @ W_res1[l] + b_res1[l]) @ W_res2[l] + b_res2[l])
        m = ssp(m)
        return u * x + (m @ W_out + b_out)
    x = _layernorm(x + _L0_gnn_ref(x, edge_attr_64, src, dst, L0_gnn_W_k2f, L0_gnn_W_i, L0_gnn_b_i, L0_gnn_W_j, L0_gnn_b_j, L0_gnn_W_res1, L0_gnn_b_res1, L0_gnn_W_res2, L0_gnn_b_res2, L0_gnn_W_out, L0_gnn_b_out, L0_gnn_u), axis=-1)
    return x

_drawn_inputs = setup_inputs


def setup_inputs(seed=0):
    import zlib

    import numpy as np

    out = dict(_drawn_inputs(seed))
    spreads = {'L0_gnn_b_i': (0.0, 0.555),
     'L0_gnn_b_j': (0.0, 0.8),
     'L0_gnn_b_res1': (0.0, 0.337),
     'L0_gnn_b_res2': (0.0, 0.1),
     'L0_gnn_b_out': (0.0, 0.1),
     'L0_gnn_u': (1.0, 0.2)}
    factors = {'edge_attr_64': 4.982}
    for name, (base, spread) in spreads.items():
        noise = np.random.default_rng([zlib.crc32(name.encode()), seed]).standard_normal(out[name].shape)
        drawn = base * np.exp(spread * noise) if base else spread * noise
        out[name] = jnp.asarray(drawn.astype(out[name].dtype))
    for name, factor in factors.items():
        out[name] = (out[name] * factor).astype(out[name].dtype)
    return out
```

```python
import math

import concourse.bass as bass
from concourse import mybir
from contextlib import ExitStack

F = 128
LN2 = math.log(2.0)
CAP = 40.0
EPS = 1e-5


def gnn_kernel(nc, x, src, dst, edge_attr, w_k2f, w_i, b_i, w_j, b_j, w_res1, b_res1, w_res2, b_res2,
               w_out, b_out, u, out):
    fp32 = mybir.dt.float32
    i32 = mybir.dt.int32
    u32 = mybir.dt.uint32
    ALU = mybir.AluOpType
    ACT = mybir.ActivationFunctionType

    N = x.shape[0]
    E, K = edge_attr.shape
    NRES = w_res1.shape[0]

    GROUP = 1024
    TILES = GROUP // 128
    HALF = 512
    PAIR = 2 * GROUP
    PAIRS = -(-N // PAIR)
    LAST = N - PAIR
    STEPS = 3 + 2 * NRES
    PER = 2 * STEPS

    EG = 512
    ET = EG // 128
    EGROUPS = -(-E // EG)
    TAIL = E - (EGROUPS - 1) * EG
    TAILP = TAIL // ET
    assert TAIL % ET == 0 and EGROUPS % 2 == 1
    DUMP = N + 1
    ZROWS = 22
    ZCHUNKS = -(-(DUMP + EG) // (128 * ZROWS))
    ACC_ROWS = 128 * ZROWS * ZCHUNKS

    acc = nc.dram_tensor("message_sums", (ACC_ROWS, F), fp32, kind="Internal").ap()
    acc_z = acc.rearrange("(p r) f -> p (r f)", p=128)

    ctx = ExitStack()
    with ctx:
        def sb(name, shape, dt=fp32):
            return ctx.enter_context(nc.sbuf_tensor(name, shape, dt))

        def sem(name):
            return ctx.enter_context(nc.semaphore(name))

        ident = sb("ident", [128, 128])
        negln2 = sb("negln2", [128, 128])
        ones_row = sb("ones_row", [1, 128])
        w1 = sb("w1", [128, NRES, F])
        w2 = sb("w2", [128, NRES, F])
        wi = sb("wi", [128, F])
        wj = sb("wj", [128, F])
        wo = sb("wo", [128, F])
        wk = sb("wk", [K, F])
        braw = sb("braw", [128, 1 + 2 * NRES])
        bias = sb("bias", [128, 2 + 2 * NRES])
        bj_raw = sb("bj_raw", [1, F])
        bj = sb("bj", [1, F])
        bo_raw = sb("bo_raw", [128, F])
        bo = sb("bo", [128, F])
        u1 = sb("u1", [128, F])
        zeros = sb("zeros", [128, ZROWS * F])
        dst_i = sb("dst_i", [128, EGROUPS * ET], i32)
        src_i = sb("src_i", [128, EGROUPS * ET], i32)
        src_f = sb("src_f", [128, EGROUPS * ET])
        dump_i = sb("dump_i", [128, EGROUPS * ET], i32)
        dump_f = sb("dump_f", [128, ET])
        diff_f = sb("diff_f", [128, EGROUPS * ET])
        mask = sb("mask", [128, ET, ET, 128])
        dst_now = sb("dst_now", [128, 2, ET], i32)
        xe = sb("xe", [128, 2, ET, F])
        attr = sb("attr", [128, 2, ET, K])
        srow = sb("srow", [128, 2, EG], i32)
        srow_tail = sb("srow_tail", [128, EG], i32)
        ee = sb("ee", [128, 2, EG])
        te = sb("te", [128, 2, EG])
        xaT = sb("xaT", [128, 2, EG])
        attrT = sb("attrT", [K, 2, EG])
        xjf = sb("xjf", [128, EG])
        pxj = sb("pxj", [128, 2, EG])
        same = sb("same", [128, 2, ET, ET, 128])
        cnt = sb("cnt", [128, 2, ET])
        sel = sb("sel", [128, ET])
        rows = sb("rows", [128, 2, ET], u32)
        comb = sb("comb", [128, 2, EG])
        x_nat = sb("x_nat", [128, 2, TILES, F])
        xj_nat = sb("xj_nat", [128, 2, TILES, F])
        z = sb("z", [128, 2, TILES, F])
        e = sb("e", [128, 2, GROUP])
        t = sb("t", [128, 2, GROUP])
        ug = sb("ug", [128, 2, GROUP])
        stats = sb("stats", [128, 2, TILES, 6])
        mv = sb("mv", [128, 2, TILES, 2])
        veps = sb("veps", [128, 2, TILES])
        mhalf = sb("mhalf", [128, TILES])
        minus1 = sb("minus1", [128, TILES])
        epsv = sb("epsv", [128, TILES])
        rstd = sb("rstd", [128, 2, TILES])
        nmr = sb("nmr", [128, 2, TILES])

        ps = ctx.enter_context(nc.psum_tensor("ps", [128, 8, 512], fp32))

        s_w = sem("weights_loaded")
        s_idx = sem("indices_loaded")
        s_pad = sem("padding_set")
        s_const = sem("constants_made")
        s_cdve = sem("constants_dve")
        s_bps = sem("bias_sums_ready")
        s_bias = sem("biases_ready")
        s_zero = sem("zeros_ready")
        s_zf = sem("table_zeroed")
        s_ga = [sem("gathered_even"), sem("gathered_odd")]
        s_la = [sem("edge_loads_even"), sem("edge_loads_odd")]
        s_pass = sem("pool_passed")
        s_dpass = sem("vector_passed")
        s_now = sem("gather_indices_ready")
        s_xT = sem("edge_xT")
        s_aT = sem("edge_attrT")
        s_aTs = sem("edge_attrT_sbuf")
        s_ex = sem("edge_exp")
        s_ln = sem("edge_ln")
        s_xa = sem("edge_xa_ready")
        s_J = sem("edge_J_ready")
        s_G = sem("edge_G_ready")
        s_ex2 = sem("edge_exp2")
        s_ln2 = sem("edge_ln2")
        s_xjf = sem("edge_xjf")
        s_px = sem("edge_pxj_ready")
        s_same = sem("edge_same_ready")
        s_sel = sem("edge_sel")
        s_rows = sem("edge_rows_ready")
        s_D = sem("edge_D_ready")
        s_comb = sem("edge_comb_ready")
        s_sc = sem("scattered")

        s_x = [sem("x_loaded_A"), sem("x_loaded_B")]
        s_xj = [sem("xj_loaded_A"), sem("xj_loaded_B")]
        s_pe = sem("product_ready")
        s_exp = sem("exp_ready")
        s_log = sem("log_ready")
        s_min = sem("capped")
        s_u = sem("softplus_ready")
        s_o = sem("output_product_ready")
        s_z = sem("z_ready")
        s_st = sem("stats_ready")
        s_mv = sem("mean_var_ready")
        s_xm = sem("x_times_u")
        s_xu = sem("x_part_ready")
        s_ve = sem("var_eps")
        s_rs = sem("rstd_ready")
        s_nm = sem("shift_ready")
        s_norm = sem("normalised")
        s_out = [sem("stored_A"), sem("stored_B")]

        block = ctx.enter_context(nc.Block())

        NW = 12 * 16

        def bank(s, q):
            return 4 * q + (2 if s % 2 else 0)

        def edges(engine, step):
            step(0, 0, True, False, False)
            step(0, 1, True, True, False)
            with engine.Fori(1, EGROUPS // 2) as k:
                step(k, 0, True, True, True)
                step(k, 1, True, True, True)
            k = EGROUPS // 2
            step(k, 0, True, True, True)
            step(k, 1, False, True, True)
            step(k + 1, 0, False, False, True)

        @block.sync
        def _(sp):
            full = (EGROUPS - 1) * EG
            sp.wait_ge(s_pad, 1)
            for dram, tile in ((dst, dst_i), (src, src_i)):
                with nc.allow_non_contiguous_dma(reason="one row of four indices per partition and group"):
                    sp.dma_start(tile[:, 0:(EGROUPS - 1) * ET].rearrange("p (g j) -> p g j", j=ET),
                                 dram[0:full].rearrange("(g p j) -> p g j", p=128, j=ET)).then_inc(s_idx, 16)
                    sp.dma_start(tile[0:TAILP, (EGROUPS - 1) * ET:EGROUPS * ET],
                                 dram[full:E].rearrange("(p j) -> p j", j=ET)).then_inc(s_idx, 16)

            def load_edges(g, k, p, tail=False):
                if not tail:
                    sp.dma_start(attr[:, p, :, :],
                                 edge_attr[bass.ds(g * EG, EG), :].rearrange("(p j) c -> p j c", j=ET)
                                 ).then_inc(s_la[p], 16)
                    sp.dma_start(srow[:, p, :],
                                 src[bass.ds(g * EG, EG)].rearrange("(o e) -> o e", o=1)
                                 .to_broadcast((128, EG))).then_inc(s_la[p], 16)
                else:
                    sp.dma_start(attr[0:TAILP, p, :, :],
                                 edge_attr[full:E, :].rearrange("(p j) c -> p j c", j=ET)).then_inc(s_la[p], 16)
                    sp.dma_start(srow_tail[:, 0:TAIL],
                                 src[full:E].rearrange("(o e) -> o e", o=1)
                                 .to_broadcast((128, TAIL))).then_inc(s_la[p], 16)

            load_edges(0, 0, 0)
            load_edges(1, 0, 1)
            sp.dma_start(wi[:, :], w_i).then_inc(s_w, 16)
            sp.dma_start(wj[:, :], w_j).then_inc(s_w, 16)
            sp.dma_start(wo[:, :], w_out).then_inc(s_w, 16)
            sp.dma_start(wk[:, :], w_k2f).then_inc(s_w, 16)
            sp.dma_start(w1[:, :, :], w_res1.rearrange("l k f -> k l f")).then_inc(s_w, 16)
            sp.dma_start(w2[:, :, :], w_res2.rearrange("l k f -> k l f")).then_inc(s_w, 16)
            with nc.allow_non_contiguous_dma(reason="bias columns, once"):
                sp.dma_start(braw[:, 0:1], b_i.rearrange("(f o) -> f o", o=1)).then_inc(s_w, 16)
                sp.dma_start(braw[:, 1:1 + NRES], b_res1.rearrange("l f -> f l")).then_inc(s_w, 16)
                sp.dma_start(braw[:, 1 + NRES:1 + 2 * NRES], b_res2.rearrange("l f -> f l")).then_inc(s_w, 16)
            sp.dma_start(bj_raw[:, :], b_j.rearrange("(o f) -> o f", o=1)).then_inc(s_w, 16)
            sp.dma_start(bo_raw[:, :], b_out.rearrange("(o f) -> o f", o=1).to_broadcast((128, F))).then_inc(s_w, 16)
            sp.dma_start(u1[:, :], u.rearrange("(o f) -> o f", o=1).to_broadcast((128, F))).then_inc(s_w, 16)

            def load_x(base, q):
                sp.dma_start(x_nat[:, q, :, :], x[bass.ds(base + q * GROUP, GROUP), :]
                             .rearrange("(p j) f -> p j f", j=TILES)).then_inc(s_x[q], 16)

            def load_xj(base, q):
                sp.dma_start(xj_nat[:, q, :, :], acc[bass.ds(base + q * GROUP, GROUP), :]
                             .rearrange("(p j) f -> p j f", j=TILES)).then_inc(s_xj[q], 16)

            sp.wait_ge(s_zero, 1)
            with sp.Fori(0, ZCHUNKS) as c:
                sp.dma_start(acc_z[:, bass.ds(c * (ZROWS * F), ZROWS * F)], zeros[:, :]).then_inc(s_zf, 16)

            with sp.Fori(1, EGROUPS // 2) as k:
                for p in range(2):
                    sp.wait_ge(s_aT, 2 * k + p - 1)
                    sp.wait_ge(s_same, 2 * k + p - 1)
                    load_edges(2 * k + p, k, p)
            k = EGROUPS // 2
            sp.wait_ge(s_aT, 2 * k - 1)
            sp.wait_ge(s_same, 2 * k - 1)
            load_edges(None, k, 0, tail=True)

            load_x(0, 0)
            load_x(0, 1)
            sp.wait_ge(s_sc, EGROUPS * ET * 16)
            load_xj(0, 0)
            load_xj(0, 1)

            def store(i, base, q):
                sp.wait_ge(s_norm, 2 * i + q + 1)
                sp.dma_start(out[bass.ds(base + q * GROUP, GROUP), :].rearrange("(p j) f -> p j f", j=TILES),
                             z[:, q, :, :]).then_inc(s_out[q], 16)

            def pair(i, base_next, base_before):
                if base_before is not None:
                    store(i - 1, base_before, 0)
                    store(i - 1, base_before, 1)
                for q in range(2):
                    sp.wait_ge(s_xm, 2 * i + q + 1)
                    sp.wait_ge(s_pe, 2 * (PER * i + q) + 2)
                    load_x(base_next, q)
                for q in range(2):
                    sp.wait_ge(s_pe, 2 * (PER * i + 4 + q) + 2)
                    load_xj(base_next, q)

            pair(0, PAIR, None)
            with sp.Fori(1, PAIRS - 2) as i:
                pair(i, (i + 1) * PAIR, (i - 1) * PAIR)
            pair(PAIRS - 2, LAST, (PAIRS - 3) * PAIR)
            store(PAIRS - 2, (PAIRS - 2) * PAIR, 0)
            store(PAIRS - 2, (PAIRS - 2) * PAIR, 1)
            sp.wait_ge(s_out[0], 16 * (PAIRS - 1))
            sp.wait_ge(s_out[1], 16 * (PAIRS - 1))
            store(PAIRS - 1, LAST, 0)
            store(PAIRS - 1, LAST, 1)
            sp.wait_ge(s_out[0], 16 * PAIRS)
            sp.wait_ge(s_out[1], 16 * PAIRS)

        @block.gpsimd
        def _(pool):
            nc.gpsimd.memset(dst_i[:, (EGROUPS - 1) * ET:], 0)
            nc.gpsimd.memset(srow_tail[:, :], N)
            nc.gpsimd.memset(src_i[:, (EGROUPS - 1) * ET:], N).then_inc(s_pad, 1)
            nc.gpsimd.memset(zeros[:, :], 0.0).then_inc(s_zero, 1)
            nc.gpsimd.memset(ident[:, :], 0.0).then_inc(s_const, 1)
            nc.gpsimd.memset(negln2[:, :], -LN2)
            nc.gpsimd.memset(ones_row[:, :], 1.0)
            nc.gpsimd.memset(mhalf[:, :], -0.5)
            nc.gpsimd.memset(minus1[:, :], -1.0)
            nc.gpsimd.memset(epsv[:, :], EPS)
            nc.gpsimd.memset(mask[:, :, :, :], 1.0).then_inc(s_const, 1)
            nc.gpsimd.iota(dump_i[:, :].rearrange("p (g j) -> p g j", j=ET), pattern=[[0, EGROUPS], [128, ET]],
                           base=DUMP, channel_multiplier=1)
            pool.wait_ge(s_const, 1)
            nc.gpsimd.affine_select(out=ident[:, :], in_=ident[:, :], compare_op=ALU.not_equal, fill=1.0, base=0,
                                    pattern=[[-1, 128]], channel_multiplier=1)
            pool.wait_ge(s_const, 2)
            for j in range(ET):
                last = nc.gpsimd.affine_select(out=mask[:, j, :, :], in_=mask[:, j, :, :], compare_op=ALU.is_ge,
                                               fill=0.0, base=j, pattern=[[-1, ET], [-ET, 128]],
                                               channel_multiplier=ET)
            last.then_inc(s_const, 1)
            pool.wait_ge(s_idx, 64)

            def gather(g, p):
                nc.gpsimd.tensor_copy(dst_now[:, p, :], dst_i[:, bass.ds(g * ET, ET)]).then_inc(s_now, 1)
                pool.wait_ge(s_now, g + 1)
                pool.sem_inc(s_pass, 1)
                for j in range(ET):
                    nc.gpsimd.indirect_dma_start(
                        out=xe[:, p, j, :], out_offset=None, in_=x,
                        in_offset=bass.IndirectOffsetOnAxis(ap=dst_now[:, p, j:j + 1], axis=0)
                    ).then_inc(s_ga[p], 16)

            gather(0, 0)

            def step(k, p, front, mid, back):
                g = 2 * k + p
                if front and not (isinstance(k, int) and k == EGROUPS // 2):
                    if not (isinstance(g, int) and g == 0):
                        pool.wait_ge(s_xT, g)
                    gather(g + 1, (p + 1) % 2)
                if back:
                    c = g - 2
                    pool.wait_ge(s_zf, 16 * ZCHUNKS)
                    pool.wait_ge(s_comb, c + 1)
                    if not (isinstance(c, int) and c == 0):
                        pool.wait_ge(s_sc, 16 * ET * c)
                    pool.sem_inc(s_pass, 1)
                    for j in range(ET):
                        nc.gpsimd.indirect_dma_start(
                            out=acc, out_offset=bass.IndirectOffsetOnAxis(ap=rows[:, p, j:j + 1], axis=0),
                            in_=comb[:, p, j * F:(j + 1) * F], in_offset=None,
                            compute_op=ALU.add).then_inc(s_sc, 16)

            edges(pool, step)

            def x_part(i, q):
                pool.wait_ge(s_x[q], 16 * (i + 1))
                if not (isinstance(i, int) and i == 0):
                    pool.wait_ge(s_out[q], 16 * i)
                nc.gpsimd.tensor_tensor(out=z[:, q, :, :], in0=x_nat[:, q, :, :],
                                        in1=u1[:, :].unsqueeze(1).to_broadcast((128, TILES, F)),
                                        op=ALU.mult).then_inc(s_xm, 1)
                pool.wait_ge(s_xm, 2 * i + q + 1)
                nc.gpsimd.tensor_tensor(out=z[:, q, :, :], in0=z[:, q, :, :],
                                        in1=bo[:, :].unsqueeze(1).to_broadcast((128, TILES, F)),
                                        op=ALU.add).then_inc(s_xu, 1)

            def normalise(i, q):
                n = 2 * i + q + 1
                pool.wait_ge(s_const, 3)
                pool.wait_ge(s_mv, n)
                nc.gpsimd.tensor_tensor(out=veps[:, q, :], in0=mv[:, q, :, 1], in1=epsv[:, :],
                                        op=ALU.add).then_inc(s_ve, 1)
                pool.wait_ge(s_ve, n)
                nc.gpsimd.tensor_tensor(out=rstd[:, q, :], in0=veps[:, q, :], in1=mhalf[:, :],
                                        op=ALU.pow).then_inc(s_rs, 1)
                pool.wait_ge(s_rs, n)
                nc.gpsimd.tensor_tensor(out=nmr[:, q, :], in0=mv[:, q, :, 0], in1=rstd[:, q, :],
                                        op=ALU.mult).then_inc(s_nm, 1)
                pool.wait_ge(s_nm, 2 * n - 1)
                nc.gpsimd.tensor_tensor(out=nmr[:, q, :], in0=nmr[:, q, :], in1=minus1[:, :],
                                        op=ALU.mult).then_inc(s_nm, 1)
                pool.wait_ge(s_nm, 2 * n)
                pool.sem_inc(s_pass, 1)
                for j in range(TILES):
                    last = nc.gpsimd.tensor_scalar(z[:, q, j, :], z[:, q, j, :], rstd[:, q, j:j + 1],
                                                   nmr[:, q, j:j + 1], ALU.mult, ALU.add)
                last.then_inc(s_norm, 1)

            pool.wait_ge(s_bias, 1)
            x_part(0, 0)
            x_part(0, 1)
            with pool.Fori(1, PAIRS) as i:
                normalise(i - 1, 0)
                normalise(i - 1, 1)
                x_part(i, 0)
                x_part(i, 1)
            normalise(PAIRS - 1, 0)
            normalise(PAIRS - 1, 1)

        @block.scalar
        def _(act):
            nc.scalar.preload_act_table_set("natural_log_exp_and_others")

            def step(k, p, front, mid, back):
                g = 2 * k + p
                if front:
                    act.wait_ge(s_xT, g + 1)
                    if not (isinstance(g, int) and g == 0):
                        act.wait_ge(s_ln, g)
                    nc.scalar.activation(ee[:, 0, :], ps[:, p, :], ACT.Exp).then_inc(s_ex, 1)
                    act.wait_ge(s_ex, g + 1)
                    if not (isinstance(g, int) and g == 0):
                        act.wait_ge(s_xa, g)
                    nc.scalar.activation(te[:, 0, :], ee[:, 0, :], ACT.Ln, bias=1.0).then_inc(s_ln, 1)
                if mid:
                    m, pm = g - 1, (p + 1) % 2
                    act.wait_ge(s_J, m + 1)
                    if not (isinstance(m, int) and m == 0):
                        act.wait_ge(s_ln2, m)
                    nc.scalar.activation(ee[:, 1, :], ps[:, 2 + pm, :], ACT.Exp).then_inc(s_ex2, 1)
                    act.wait_ge(s_ex2, m + 1)
                    if not (isinstance(m, int) and m == 0):
                        act.wait_ge(s_xjf, m)
                    nc.scalar.activation(te[:, 1, :], ee[:, 1, :], ACT.Ln, bias=1.0).then_inc(s_ln2, 1)

            edges(act, step)

            act.wait_ge(s_bias, 1)

            def softplus(i, s, q):
                n = PER * i + 2 * s + q
                lo = bank(s, q)
                for h in range(2):
                    act.wait_ge(s_pe, 2 * n + h + 1)
                    kw = {} if s == 0 else {"bias": bias[:, s - 1:s]}
                    nc.scalar.activation(e[:, q, h * HALF:(h + 1) * HALF], ps[:, lo + h, :], ACT.Exp,
                                         **kw).then_inc(s_exp, 1)
                for h in range(2):
                    act.wait_ge(s_exp, 2 * n + h + 1)
                    nc.scalar.activation(t[:, q, h * HALF:(h + 1) * HALF], e[:, q, h * HALF:(h + 1) * HALF],
                                         ACT.Ln, bias=1.0).then_inc(s_log, 1)

            with act.Fori(0, PAIRS) as i:
                for s in range(STEPS):
                    for q in range(2):
                        softplus(i, s, q)

        @block.vector
        def _(dve):
            dve.wait_ge(s_w, NW)
            nc.vector.tensor_scalar(u1[:, :], u1[:, :], 1.0, None, ALU.add)
            dve.wait_ge(s_idx, 64)
            nc.vector.tensor_copy(src_f[:, :], src_i[:, :]).then_inc(s_cdve, 1)
            dve.wait_ge(s_const, 3)
            nc.vector.tensor_copy(dump_f[:, :], dump_i[:, 0:ET])
            dve.wait_ge(s_cdve, 1)
            nc.vector.tensor_tensor(out=diff_f[:, :], in0=src_f[:, :], in1=dump_i[:, :],
                                    op=ALU.subtract).then_inc(s_cdve, 1)
            dve.wait_ge(s_cdve, 2)
            dve.wait_ge(s_bps, 1)
            nc.vector.tensor_tensor(out=bias[:, 0:1], in0=ps[:, 7, 0:1], in1=braw[:, 0:1], op=ALU.add)
            nc.vector.memset(bias[:, 1:2], -LN2).then_inc(s_cdve, 1)
            nc.vector.tensor_tensor(out=bj[:, :], in0=ps[0:1, 7, 128:256], in1=bj_raw[:, :], op=ALU.add)
            nc.vector.tensor_tensor(out=bo[:, :], in0=ps[:, 7, 256:384], in1=bo_raw[:, :], op=ALU.add)
            for l in range(NRES):
                nc.vector.tensor_tensor(out=bias[:, 2 + 2 * l:3 + 2 * l], in0=ps[:, 7, 1 + l:2 + l],
                                        in1=braw[:, 1 + l:2 + l], op=ALU.add)
                dve.wait_ge(s_cdve, 3 + l)
                nc.vector.scalar_tensor_tensor(out=bias[:, 3 + 2 * l:4 + 2 * l],
                                               in0=ps[:, 7, 1 + NRES + l:2 + NRES + l],
                                               scalar=braw[:, 1 + NRES + l:2 + NRES + l],
                                               in1=bias[:, 1 + 2 * l:2 + 2 * l],
                                               op0=ALU.add, op1=ALU.add).then_inc(s_cdve, 1)
            dve.wait_ge(s_cdve, 3 + NRES)
            nc.vector.tensor_copy(bias[:, 0:1], bias[:, 0:1]).then_inc(s_bias, 1)

            def step(k, p, front, mid, back):
                g = 2 * k + p
                if front:
                    dve.wait_ge(s_aT, g + 1)
                    nc.vector.tensor_copy(attrT[:, p, :], ps[0:K, 4, :]).then_inc(s_aTs, 1)
                    dve.wait_ge(s_ln, g + 1)
                    nc.vector.scalar_tensor_tensor(out=xaT[:, p, :], in0=te[:, 0, :], scalar=CAP,
                                                   in1=ps[:, p, :], op0=ALU.min, op1=ALU.max).then_inc(s_xa, 1)
                if mid:
                    m, pm = g - 1, (p + 1) % 2
                    km = (m - pm) // 2 if isinstance(m, int) else (k if pm == 0 else k - 1)
                    dve.wait_ge(s_la[pm], 32 * (km + 1))
                    targets = srow_tail[:, :] if isinstance(m, int) and m == EGROUPS - 1 else srow[:, pm, :]
                    for j in range(ET):
                        col = 4 * m + j
                        last = nc.vector.scalar_tensor_tensor(
                            out=same[:, pm, j, :, :],
                            in0=targets.rearrange("p (c j) -> p j c", j=ET),
                            scalar=src_f[:, bass.ds(col, 1)], in1=mask[:, j, :, :],
                            op0=ALU.is_equal, op1=ALU.mult, accum_out=cnt[:, pm, j:j + 1])
                    last.then_inc(s_same, 1)
                if back:
                    c = g - 2
                    dve.wait_ge(s_D, c + 1)
                    nc.vector.tensor_copy(comb[:, p, :], ps[:, 6, :]).then_inc(s_comb, 1)
                if mid:
                    dve.wait_ge(s_same, m + 1)
                    nc.vector.scalar_tensor_tensor(out=sel[:, :], in0=cnt[:, pm, :], scalar=1.0,
                                                   in1=diff_f[:, bass.ds(4 * m, ET)],
                                                   op0=ALU.is_equal, op1=ALU.mult).then_inc(s_sel, 1)
                    dve.wait_ge(s_ln2, m + 1)
                    nc.vector.scalar_tensor_tensor(out=xjf[:, :], in0=te[:, 1, :], scalar=CAP,
                                                   in1=ps[:, 2 + pm, :], op0=ALU.min,
                                                   op1=ALU.max).then_inc(s_xjf, 1)
                    dve.wait_ge(s_sel, m + 1)
                    if not (isinstance(m, int) and m < 2):
                        dve.wait_ge(s_sc, 16 * ET * (m - 1))
                    nc.vector.tensor_tensor(out=rows[:, pm, :], in0=sel[:, :], in1=dump_f[:, :],
                                            op=ALU.add).then_inc(s_rows, 1)
                    dve.wait_ge(s_xjf, m + 1)
                    dve.wait_ge(s_G, m + 1)
                    nc.vector.scalar_tensor_tensor(out=pxj[:, pm, :], in0=xjf[:, :], scalar=-LN2,
                                                   in1=ps[:, 5, :], op0=ALU.add,
                                                   op1=ALU.mult).then_inc(s_px, 1)

            edges(dve, step)

            def softplus(i, s, q):
                n = PER * i + 2 * s + q
                lo = bank(s, q)
                if s == 0:
                    if not (isinstance(i, int) and i == 0):
                        dve.wait_ge(s_o, 2 * (2 * (i - 1) + q) + 2)
                    for h in range(2):
                        dve.wait_ge(s_log, 2 * n + h + 1)
                        half = slice(h * HALF, (h + 1) * HALF)
                        nc.vector.scalar_tensor_tensor(out=ug[:, q, half], in0=t[:, q, half], scalar=CAP,
                                                       in1=ps[:, lo + h, :], op0=ALU.min,
                                                       op1=ALU.max).then_inc(s_u, 1)
                    return
                nm = (PER - 2) * i + 2 * (s - 1) + q
                for h in range(2):
                    dve.wait_ge(s_log, 2 * n + h + 1)
                    half = slice(h * HALF, (h + 1) * HALF)
                    nc.vector.tensor_scalar(t[:, q, half], t[:, q, half], CAP, None, ALU.min).then_inc(s_min, 1)
                for h in range(2):
                    half = slice(h * HALF, (h + 1) * HALF)
                    dve.wait_ge(s_min, 2 * nm + h + 1)
                    nc.vector.scalar_tensor_tensor(out=ug[:, q, half], in0=ps[:, lo + h, :],
                                                   scalar=bias[:, s - 1:s], in1=t[:, q, half],
                                                   op0=ALU.add, op1=ALU.max).then_inc(s_u, 1)

            def finish(i, q):
                n = 2 * i + q
                dve.wait_ge(s_xu, n + 1)
                for h in range(2):
                    dve.wait_ge(s_o, 2 * n + h + 1)
                    zh = z[:, q, 4 * h:4 * h + 4, :]
                    nc.vector.tensor_tensor(out=zh, in0=ps[:, 4 * q + 2 + h, :].rearrange("p (j f) -> p j f", f=F),
                                            in1=zh, op=ALU.add).then_inc(s_z, 1)
                for h in range(2):
                    dve.wait_ge(s_z, 2 * n + h + 1)
                    for j in range(4 * h, 4 * h + 4):
                        last = nc.vector.bn_stats(stats[:, q, j, :], z[:, q, j, :])
                last.then_inc(s_st, 1)
                dve.wait_ge(s_st, n + 1)
                dve.sem_inc(s_dpass, 1)
                for j in range(TILES):
                    last = nc.vector.bn_aggr(mv[:, q, j, :], stats[:, q, j, :])
                last.then_inc(s_mv, 1)

            def pair(i, first=False):
                for q in range(2):
                    softplus(i, 0, q)
                    if not first:
                        finish(i - 1, q)
                for s in range(1, STEPS):
                    for q in range(2):
                        softplus(i, s, q)

            pair(0, first=True)
            with dve.Fori(1, PAIRS) as i:
                pair(i)
            finish(PAIRS - 1, 0)
            finish(PAIRS - 1, 1)

        @block.tensor
        def _(pe):
            pe.wait_ge(s_w, NW)
            pe.wait_ge(s_const, 3)
            cols = [wi[:, :]] + [w1[:, l, :] for l in range(NRES)] + [w2[:, l, :] for l in range(NRES)]
            for c, w in enumerate(cols):
                nc.tensor.matmul(ps[:, 7, c:c + 1], w, negln2[:, 0:1], start=True, stop=True)
            nc.tensor.matmul(ps[:, 7, 128:256], negln2[:, :], wj[:, :], start=True, stop=True)
            nc.tensor.matmul(ps[:, 7, 256:384], negln2[:, :], wo[:, :], start=True, stop=True).then_inc(s_bps, 1)
            pe.wait_ge(s_bias, 1)

            def step(k, p, front, mid, back):
                g = 2 * k + p
                if front:
                    pe.wait_ge(s_ga[p], 16 * ET * (k + 1))
                    pe.wait_ge(s_la[p], 32 * (k + 1))
                    if not (isinstance(g, int) and g == 0):
                        pe.wait_ge(s_aTs, g)
                    for j in range(ET):
                        last = nc.tensor.transpose(ps[:, p, j * 128:(j + 1) * 128], xe[:, p, j, :], ident[:, :])
                    last.then_inc(s_xT, 1)
                    for j in range(ET):
                        last = nc.tensor.transpose(ps[0:K, 4, j * 128:(j + 1) * 128], attr[:, p, j, :], ident[:, :])
                    last.then_inc(s_aT, 1)
                if back:
                    c = g - 2
                    pe.wait_ge(s_px, c + 1)
                    pe.wait_ge(s_same, c + 1)
                    if not (isinstance(c, int) and c == 0):
                        pe.wait_ge(s_comb, c)
                    for j in range(ET):
                        for jj in range(ET):
                            last = nc.tensor.matmul(ps[:, 6, j * F:(j + 1) * F], same[:, p, jj, j, :],
                                                    pxj[:, p, jj * F:(jj + 1) * F],
                                                    start=(jj == 0), stop=(jj == ET - 1))
                    last.then_inc(s_D, 1)
                if mid:
                    m, pm = g - 1, (p + 1) % 2
                    pe.wait_ge(s_xa, m + 1)
                    for j in range(ET):
                        o = ps[:, 2 + pm, j * F:(j + 1) * F]
                        nc.tensor.matmul(o, xaT[:, pm, j * 128:(j + 1) * 128], wj[:, :], start=True, stop=False)
                        last = nc.tensor.matmul(o, ones_row[:, :], bj[:, :], start=False, stop=True)
                    last.then_inc(s_J, 1)
                    pe.wait_ge(s_aTs, m + 1)
                    for j in range(ET):
                        last = nc.tensor.matmul(ps[:, 5, j * F:(j + 1) * F], attrT[:, pm, j * 128:(j + 1) * 128],
                                                wk[:, :], start=True, stop=True)
                    last.then_inc(s_G, 1)

            edges(pe, step)
            pe.wait_ge(s_comb, EGROUPS)

            def layer(i, s, q):
                n = PER * i + 2 * s + q
                lo = bank(s, q)
                if s == 0:
                    pe.wait_ge(s_x[q], 16 * (i + 1))
                    if not (isinstance(i, int) and i == 0):
                        pe.wait_ge(s_u, 2 * (n - 2) + 2)
                    for h in range(2):
                        for j in range(4):
                            last = nc.tensor.transpose(ps[:, lo + h, j * 128:(j + 1) * 128],
                                                       x_nat[:, q, 4 * h + j, :], ident[:, :])
                        last.then_inc(s_pe, 1)
                    return
                if s == 1 and not (isinstance(i, int) and i == 0):
                    pe.wait_ge(s_z, 2 * (2 * (i - 1) + q) + 2)
                if s == 2:
                    pe.wait_ge(s_xj[q], 16 * (i + 1))
                    for h in range(2):
                        for j in range(4):
                            nc.tensor.matmul(ps[:, lo + h, j * 128:(j + 1) * 128], xj_nat[:, q, 4 * h + j, :],
                                             ident[:, :], is_transpose=True, start=(j == 0), stop=True,
                                             skip_group_check=True)
                w = (wi[:, :] if s == 1 else ident[:, :] if s == 2 else
                     w1[:, (s - 3) // 2, :] if s % 2 else w2[:, (s - 4) // 2, :])
                for h in range(2):
                    pe.wait_ge(s_u, 2 * (n - 2) + h + 1)
                    nc.tensor.matmul(ps[:, lo + h, :], w, ug[:, q, h * HALF:(h + 1) * HALF],
                                     start=bool(s % 2), stop=True,
                                     skip_group_check=not s % 2).then_inc(s_pe, 1)

            def output(i, q):
                n = PER * i + 2 * (STEPS - 1) + q
                for h in range(2):
                    pe.wait_ge(s_u, 2 * n + h + 1)
                    for j in range(4):
                        c = 4 * h + j
                        last = nc.tensor.matmul(ps[:, 4 * q + 2 + h, j * F:(j + 1) * F],
                                                ug[:, q, c * 128:(c + 1) * 128], wo[:, :], start=True, stop=True)
                    last.then_inc(s_o, 1)

            def pair(i, first=False):
                for q in range(2):
                    layer(i, 0, q)
                    if not first:
                        output(i - 1, q)
                for s in range(1, STEPS):
                    for q in range(2):
                        layer(i, s, q)

            pair(0, first=True)
            with pe.Fori(1, PAIRS) as i:
                pair(i)
            output(PAIRS - 1, 0)
            output(PAIRS - 1, 1)


_INS = ['x', 'src', 'dst', 'edge_attr_64', 'L0_gnn_W_k2f', 'L0_gnn_W_i', 'L0_gnn_b_i', 'L0_gnn_W_j', 'L0_gnn_b_j',
        'L0_gnn_W_res1', 'L0_gnn_b_res1', 'L0_gnn_W_res2', 'L0_gnn_b_res2', 'L0_gnn_W_out', 'L0_gnn_b_out',
        'L0_gnn_u']


def kernel(**inputs):
    import numpy as _np
    import concourse.bacc as _bacc
    from concourse import mybir as _mybir
    from concourse.bass_utils import run_bass_kernel_spmd as _run

    nc = _bacc.Bacc("TRN2", target_bir_lowering=False, num_devices=1)
    arrays, args = {}, []
    for name in _INS:
        a = _np.ascontiguousarray(inputs[name])
        arrays[f"in_{name}_dram"] = a
        args.append(nc.dram_tensor(f"in_{name}_dram", a.shape, _mybir.dt.from_np(a.dtype), kind="ExternalInput").ap())
    shape = inputs['x'].shape
    args.append(nc.dram_tensor("out_0_dram", shape, _mybir.dt.float32, kind="ExternalOutput").ap())
    gnn_kernel(nc, *args)
    r = _run(nc, [arrays], core_ids=[0])
    return r.results[0]["out_0_dram"]
```

```python
import math

import concourse.bass as bass
from concourse import mybir
from contextlib import ExitStack

F = 128
LN2 = math.log(2.0)
CAP = 40.0
LIMIT = 16.0
EPS = 1e-5


def gnn_kernel(nc, x, src, dst, edge_attr, w_k2f, w_i, b_i, w_j, b_j, w_res1, b_res1, w_res2, b_res2,
               w_out, b_out, u, out):
    fp32 = mybir.dt.float32
    i32 = mybir.dt.int32
    u32 = mybir.dt.uint32
    ALU = mybir.AluOpType
    ACT = mybir.ActivationFunctionType

    N = x.shape[0]
    E, K = edge_attr.shape
    NRES = w_res1.shape[0]

    GROUP = 1024
    TILES = GROUP // 128
    HALF = 512
    PAIR = 2 * GROUP
    PAIRS = -(-N // PAIR)
    LAST = N - PAIR
    STEPS = 3 + 2 * NRES
    LN_PARTS = 2
    EXP_PARTS = 2
    PER = 2 * STEPS

    EG = 512
    ET = EG // 128
    EGROUPS = -(-E // EG)
    TAIL = E - (EGROUPS - 1) * EG
    TAILP = TAIL // ET
    assert TAIL % ET == 0 and EGROUPS % 2 == 1
    DUMP = N + 1
    ZROWS = 22
    ZCHUNKS = -(-(DUMP + EG) // (128 * ZROWS))
    ACC_ROWS = 128 * ZROWS * ZCHUNKS

    acc = nc.dram_tensor("message_sums", (ACC_ROWS, F), fp32, kind="Internal").ap()
    acc_z = acc.rearrange("(p r) f -> p (r f)", p=128)

    ctx = ExitStack()
    with ctx:
        def sb(name, shape, dt=fp32):
            return ctx.enter_context(nc.sbuf_tensor(name, shape, dt))

        def sem(name):
            return ctx.enter_context(nc.semaphore(name))

        ident = sb("ident", [128, 128])
        negln2 = sb("negln2", [128, 128])
        ones_row = sb("ones_row", [1, 128])
        w1 = sb("w1", [128, NRES, F])
        w2 = sb("w2", [128, NRES, F])
        wi = sb("wi", [128, F])
        wj = sb("wj", [128, F])
        wo = sb("wo", [128, F])
        wk = sb("wk", [K, F])
        braw = sb("braw", [128, 1 + 2 * NRES])
        bias = sb("bias", [128, 2 + 2 * NRES])
        less = sb("less", [128, 1 + 2 * NRES])
        expb = sb("expb", [128, 2 + 2 * NRES])
        dmat = sb("dmat", [128, 128])
        bi_raw = sb("bi_raw", [128, F])
        amax = sb("amax", [128, 1])
        gmax = sb("gmax", [1, 1])
        flag = sb("flag", [1, 1], i32)
        bj_raw = sb("bj_raw", [1, F])
        bj = sb("bj", [1, F])
        bo_raw = sb("bo_raw", [128, F])
        bo = sb("bo", [128, F])
        u1 = sb("u1", [128, F])
        zeros = sb("zeros", [128, ZROWS * F])
        dst_i = sb("dst_i", [128, EGROUPS * ET], i32)
        src_i = sb("src_i", [128, EGROUPS * ET], i32)
        src_f = sb("src_f", [128, EGROUPS * ET])
        dump_i = sb("dump_i", [128, EGROUPS * ET], i32)
        dump_f = sb("dump_f", [128, ET])
        diff_f = sb("diff_f", [128, EGROUPS * ET])
        mask = sb("mask", [128, ET, ET, 128])
        dst_now = sb("dst_now", [128, 2, ET], i32)
        xe = sb("xe", [128, 2, ET, F])
        attr = sb("attr", [128, 2, ET, K])
        srow = sb("srow", [128, 2, EG], i32)
        srow_tail = sb("srow_tail", [128, EG], i32)
        ee = sb("ee", [128, 2, EG])
        te = sb("te", [128, 2, EG])
        xaT = sb("xaT", [128, 2, EG])
        attrT = sb("attrT", [K, 2, EG])
        xjf = sb("xjf", [128, EG])
        pxj = sb("pxj", [128, 2, EG])
        same = sb("same", [128, 2, ET, ET, 128])
        cnt = sb("cnt", [128, 2, ET])
        sel = sb("sel", [128, ET])
        rows = sb("rows", [128, 2, ET], u32)
        comb = sb("comb", [128, 2, EG])
        x_nat = sb("x_nat", [128, 2, TILES, F])
        xj_nat = sb("xj_nat", [128, 2, TILES, F])
        z = sb("z", [128, 2, TILES, F])
        e = sb("e", [128, 2, GROUP])
        t = sb("t", [128, 2, GROUP])
        ug = sb("ug", [128, 2, GROUP])
        stats = sb("stats", [128, 2, TILES, 6])
        mv = sb("mv", [128, 2, TILES, 2])
        veps = sb("veps", [128, 2, TILES])
        mhalf = sb("mhalf", [128, TILES])
        minus1 = sb("minus1", [128, TILES])
        epsv = sb("epsv", [128, TILES])
        rstd = sb("rstd", [128, 2, TILES])
        nmr = sb("nmr", [128, 2, TILES])

        ps = ctx.enter_context(nc.psum_tensor("ps", [128, 8, 512], fp32))

        s_w = sem("weights_loaded")
        s_idx = sem("indices_loaded")
        s_pad = sem("padding_set")
        s_const = sem("constants_made")
        s_cdve = sem("constants_dve")
        s_bps = sem("bias_sums_ready")
        s_less = sem("bias_inputs_ready")
        s_bv = sem("bias_chain")
        s_bias = sem("biases_ready")
        s_eb = sem("exp_bias_ready")
        s_zero = sem("zeros_ready")
        s_zf = sem("table_zeroed")
        s_ga = [sem("gathered_even"), sem("gathered_odd")]
        s_la = [sem("edge_loads_even"), sem("edge_loads_odd")]
        s_pass = sem("pool_passed")
        s_dpass = sem("vector_passed")
        s_now = sem("gather_indices_ready")
        s_xT = sem("edge_xT")
        s_aT = sem("edge_attrT")
        s_aTs = sem("edge_attrT_sbuf")
        s_ex = sem("edge_exp")
        s_ln = sem("edge_ln")
        s_xa = sem("edge_xa_ready")
        s_J = sem("edge_J_ready")
        s_G = sem("edge_G_ready")
        s_ex2 = sem("edge_exp2")
        s_ln2 = sem("edge_ln2")
        s_xjf = sem("edge_xjf")
        s_px = sem("edge_pxj_ready")
        s_same = sem("edge_same_ready")
        s_sel = sem("edge_sel")
        s_rows = sem("edge_rows_ready")
        s_D = sem("edge_D_ready")
        s_comb = sem("edge_comb_ready")
        s_sc = sem("scattered")

        s_x = [sem("x_loaded_A"), sem("x_loaded_B")]
        s_xj = [sem("xj_loaded_A"), sem("xj_loaded_B")]
        s_pe = sem("product_ready")
        s_exp = sem("exp_ready")
        s_log = sem("log_ready")
        s_min = sem("capped")
        s_u = sem("softplus_ready")
        s_o = sem("output_product_ready")
        s_z = sem("z_ready")
        s_st = sem("stats_ready")
        s_mv = sem("mean_var_ready")
        s_xm = sem("x_times_u")
        s_xu = sem("x_part_ready")
        s_ve = sem("var_eps")
        s_rs = sem("rstd_ready")
        s_nm = sem("shift_ready")
        s_norm = sem("normalised")
        s_out = [sem("stored_A"), sem("stored_B")]

        block = ctx.enter_context(nc.Block())

        NW = 13 * 16

        def bank(s, q):
            return 4 * q + (0 if s % 2 == 0 and s > 0 else 2)

        def edges(engine, step):
            step(0, 0, True, False, False)
            step(0, 1, True, True, False)
            with engine.Fori(1, EGROUPS // 2) as k:
                step(k, 0, True, True, True)
                step(k, 1, True, True, True)
            k = EGROUPS // 2
            step(k, 0, True, True, True)
            step(k, 1, False, True, True)
            step(k + 1, 0, False, False, True)

        @block.sync
        def _(sp):
            full = (EGROUPS - 1) * EG
            sp.wait_ge(s_pad, 1)
            for dram, tile in ((dst, dst_i), (src, src_i)):
                with nc.allow_non_contiguous_dma(reason="one row of four indices per partition and group"):
                    sp.dma_start(tile[:, 0:(EGROUPS - 1) * ET].rearrange("p (g j) -> p g j", j=ET),
                                 dram[0:full].rearrange("(g p j) -> p g j", p=128, j=ET)).then_inc(s_idx, 16)
                    sp.dma_start(tile[0:TAILP, (EGROUPS - 1) * ET:EGROUPS * ET],
                                 dram[full:E].rearrange("(p j) -> p j", j=ET)).then_inc(s_idx, 16)

            def load_edges(g, k, p, tail=False):
                if not tail:
                    sp.dma_start(attr[:, p, :, :],
                                 edge_attr[bass.ds(g * EG, EG), :].rearrange("(p j) c -> p j c", j=ET)
                                 ).then_inc(s_la[p], 16)
                    sp.dma_start(srow[:, p, :],
                                 src[bass.ds(g * EG, EG)].rearrange("(o e) -> o e", o=1)
                                 .to_broadcast((128, EG))).then_inc(s_la[p], 16)
                else:
                    sp.dma_start(attr[0:TAILP, p, :, :],
                                 edge_attr[full:E, :].rearrange("(p j) c -> p j c", j=ET)).then_inc(s_la[p], 16)
                    sp.dma_start(srow_tail[:, 0:TAIL],
                                 src[full:E].rearrange("(o e) -> o e", o=1)
                                 .to_broadcast((128, TAIL))).then_inc(s_la[p], 16)

            load_edges(0, 0, 0)
            load_edges(1, 0, 1)
            sp.dma_start(wi[:, :], w_i).then_inc(s_w, 16)
            sp.dma_start(wj[:, :], w_j).then_inc(s_w, 16)
            sp.dma_start(wo[:, :], w_out).then_inc(s_w, 16)
            sp.dma_start(wk[:, :], w_k2f).then_inc(s_w, 16)
            sp.dma_start(w1[:, :, :], w_res1.rearrange("l k f -> k l f")).then_inc(s_w, 16)
            sp.dma_start(w2[:, :, :], w_res2.rearrange("l k f -> k l f")).then_inc(s_w, 16)
            with nc.allow_non_contiguous_dma(reason="bias columns, once"):
                sp.dma_start(braw[:, 0:1], b_i.rearrange("(f o) -> f o", o=1)).then_inc(s_w, 16)
                sp.dma_start(braw[:, 1:1 + NRES], b_res1.rearrange("l f -> f l")).then_inc(s_w, 16)
                sp.dma_start(braw[:, 1 + NRES:1 + 2 * NRES], b_res2.rearrange("l f -> f l")).then_inc(s_w, 16)
            sp.dma_start(bj_raw[:, :], b_j.rearrange("(o f) -> o f", o=1)).then_inc(s_w, 16)
            sp.dma_start(bo_raw[:, :], b_out.rearrange("(o f) -> o f", o=1).to_broadcast((128, F))).then_inc(s_w, 16)
            sp.dma_start(bi_raw[:, :], b_i.rearrange("(o f) -> o f", o=1).to_broadcast((128, F))).then_inc(s_w, 16)
            sp.dma_start(u1[:, :], u.rearrange("(o f) -> o f", o=1).to_broadcast((128, F))).then_inc(s_w, 16)

            def load_x(base, q):
                sp.dma_start(x_nat[:, q, :, :], x[bass.ds(base + q * GROUP, GROUP), :]
                             .rearrange("(p j) f -> p j f", j=TILES)).then_inc(s_x[q], 16)

            def load_xj(base, q):
                sp.dma_start(xj_nat[:, q, :, :], acc[bass.ds(base + q * GROUP, GROUP), :]
                             .rearrange("(p j) f -> p j f", j=TILES)).then_inc(s_xj[q], 16)

            sp.wait_ge(s_zero, 1)
            with sp.Fori(0, ZCHUNKS) as c:
                sp.dma_start(acc_z[:, bass.ds(c * (ZROWS * F), ZROWS * F)], zeros[:, :]).then_inc(s_zf, 16)

            with sp.Fori(1, EGROUPS // 2) as k:
                for p in range(2):
                    sp.wait_ge(s_aT, 2 * k + p - 1)
                    sp.wait_ge(s_same, 2 * k + p - 1)
                    load_edges(2 * k + p, k, p)
            k = EGROUPS // 2
            sp.wait_ge(s_aT, 2 * k - 1)
            sp.wait_ge(s_same, 2 * k - 1)
            load_edges(None, k, 0, tail=True)

            load_x(0, 0)
            load_x(0, 1)
            sp.wait_ge(s_sc, EGROUPS * ET * 16)
            load_xj(0, 0)
            load_xj(0, 1)

            def store(i, base, q):
                sp.wait_ge(s_norm, 2 * i + q + 1)
                sp.dma_start(out[bass.ds(base + q * GROUP, GROUP), :].rearrange("(p j) f -> p j f", j=TILES),
                             z[:, q, :, :]).then_inc(s_out[q], 16)

            def pair(i, base_next, base_before):
                if base_before is not None:
                    store(i - 1, base_before, 0)
                    store(i - 1, base_before, 1)
                for q in range(2):
                    sp.wait_ge(s_xm, 2 * i + q + 1)
                    sp.wait_ge(s_pe, 2 * (PER * i + q) + 2)
                    load_x(base_next, q)
                for q in range(2):
                    sp.wait_ge(s_pe, 2 * (PER * i + 4 + q) + 2)
                    load_xj(base_next, q)

            pair(0, PAIR, None)
            with sp.Fori(1, PAIRS - 2) as i:
                pair(i, (i + 1) * PAIR, (i - 1) * PAIR)
            pair(PAIRS - 2, LAST, (PAIRS - 3) * PAIR)
            store(PAIRS - 2, (PAIRS - 2) * PAIR, 0)
            store(PAIRS - 2, (PAIRS - 2) * PAIR, 1)
            sp.wait_ge(s_out[0], 16 * (PAIRS - 1))
            sp.wait_ge(s_out[1], 16 * (PAIRS - 1))
            store(PAIRS - 1, LAST, 0)
            store(PAIRS - 1, LAST, 1)
            sp.wait_ge(s_out[0], 16 * PAIRS)
            sp.wait_ge(s_out[1], 16 * PAIRS)

        @block.gpsimd
        def _(pool):
            nc.gpsimd.memset(dst_i[:, (EGROUPS - 1) * ET:], 0)
            nc.gpsimd.memset(srow_tail[:, :], N)
            nc.gpsimd.memset(src_i[:, (EGROUPS - 1) * ET:], N).then_inc(s_pad, 1)
            nc.gpsimd.memset(ident[:, :], 0.0).then_inc(s_const, 1)
            nc.gpsimd.memset(negln2[:, :], -LN2)
            nc.gpsimd.memset(ones_row[:, :], 1.0)
            nc.gpsimd.memset(mhalf[:, :], -0.5)
            nc.gpsimd.memset(minus1[:, :], -1.0)
            nc.gpsimd.memset(epsv[:, :], EPS)
            nc.gpsimd.memset(mask[:, :, :, :], 1.0).then_inc(s_const, 1)
            nc.gpsimd.iota(dump_i[:, :].rearrange("p (g j) -> p g j", j=ET), pattern=[[0, EGROUPS], [128, ET]],
                           base=DUMP, channel_multiplier=1)
            pool.wait_ge(s_const, 1)
            nc.gpsimd.affine_select(out=ident[:, :], in_=ident[:, :], compare_op=ALU.not_equal, fill=1.0, base=0,
                                    pattern=[[-1, 128]], channel_multiplier=1)
            pool.wait_ge(s_const, 2)
            for j in range(ET):
                last = nc.gpsimd.affine_select(out=mask[:, j, :, :], in_=mask[:, j, :, :], compare_op=ALU.is_ge,
                                               fill=0.0, base=j, pattern=[[-1, ET], [-ET, 128]],
                                               channel_multiplier=ET)
            last.then_inc(s_const, 1)
            pool.wait_ge(s_idx, 64)

            def gather(g, p):
                nc.gpsimd.tensor_copy(dst_now[:, p, :], dst_i[:, bass.ds(g * ET, ET)]).then_inc(s_now, 1)
                pool.wait_ge(s_now, g + 1)
                pool.sem_inc(s_pass, 1)
                for j in range(ET):
                    nc.gpsimd.indirect_dma_start(
                        out=xe[:, p, j, :], out_offset=None, in_=x,
                        in_offset=bass.IndirectOffsetOnAxis(ap=dst_now[:, p, j:j + 1], axis=0)
                    ).then_inc(s_ga[p], 16)

            gather(0, 0)

            def step(k, p, front, mid, back):
                g = 2 * k + p
                if front and not (isinstance(k, int) and k == EGROUPS // 2):
                    if not (isinstance(g, int) and g == 0):
                        pool.wait_ge(s_xT, g)
                    gather(g + 1, (p + 1) % 2)
                if back:
                    c = g - 2
                    pool.wait_ge(s_zf, 16 * ZCHUNKS)
                    pool.wait_ge(s_comb, c + 1)
                    if not (isinstance(c, int) and c == 0):
                        pool.wait_ge(s_sc, 16 * ET * c)
                    pool.sem_inc(s_pass, 1)
                    for j in range(ET):
                        nc.gpsimd.indirect_dma_start(
                            out=acc, out_offset=bass.IndirectOffsetOnAxis(ap=rows[:, p, j:j + 1], axis=0),
                            in_=comb[:, p, j * F:(j + 1) * F], in_offset=None,
                            compute_op=ALU.add).then_inc(s_sc, 16)

            edges(pool, step)

            def x_part(i, q):
                pool.wait_ge(s_x[q], 16 * (i + 1))
                if not (isinstance(i, int) and i == 0):
                    pool.wait_ge(s_out[q], 16 * i)
                nc.gpsimd.tensor_tensor(out=z[:, q, :, :], in0=x_nat[:, q, :, :],
                                        in1=u1[:, :].unsqueeze(1).to_broadcast((128, TILES, F)),
                                        op=ALU.mult).then_inc(s_xm, 1)
                pool.wait_ge(s_xm, 2 * i + q + 1)
                nc.gpsimd.tensor_tensor(out=z[:, q, :, :], in0=z[:, q, :, :],
                                        in1=bo[:, :].unsqueeze(1).to_broadcast((128, TILES, F)),
                                        op=ALU.add).then_inc(s_xu, 1)

            def normalise(i, q):
                n = 2 * i + q + 1
                pool.wait_ge(s_const, 3)
                pool.wait_ge(s_mv, n)
                nc.gpsimd.tensor_tensor(out=veps[:, q, :], in0=mv[:, q, :, 1], in1=epsv[:, :],
                                        op=ALU.add).then_inc(s_ve, 1)
                pool.wait_ge(s_ve, n)
                nc.gpsimd.tensor_tensor(out=rstd[:, q, :], in0=veps[:, q, :], in1=mhalf[:, :],
                                        op=ALU.pow).then_inc(s_rs, 1)
                pool.wait_ge(s_rs, n)
                nc.gpsimd.tensor_tensor(out=nmr[:, q, :], in0=mv[:, q, :, 0], in1=rstd[:, q, :],
                                        op=ALU.mult).then_inc(s_nm, 1)
                pool.wait_ge(s_nm, 2 * n - 1)
                nc.gpsimd.tensor_tensor(out=nmr[:, q, :], in0=nmr[:, q, :], in1=minus1[:, :],
                                        op=ALU.mult).then_inc(s_nm, 1)
                pool.wait_ge(s_nm, 2 * n)
                pool.sem_inc(s_pass, 1)
                for j in range(TILES):
                    last = nc.gpsimd.tensor_scalar(z[:, q, j, :], z[:, q, j, :], rstd[:, q, j:j + 1],
                                                   nmr[:, q, j:j + 1], ALU.mult, ALU.add)
                last.then_inc(s_norm, 1)

            pool.wait_ge(s_bias, 1)
            x_part(0, 0)
            x_part(0, 1)
            with pool.Fori(1, PAIRS) as i:
                normalise(i - 1, 0)
                normalise(i - 1, 1)
                x_part(i, 0)
                x_part(i, 1)
            normalise(PAIRS - 1, 0)
            normalise(PAIRS - 1, 1)

        @block.scalar
        def _(act):
            nc.scalar.preload_act_table_set("natural_log_exp_and_others")

            def step(k, p, front, mid, back):
                g = 2 * k + p
                if front:
                    act.wait_ge(s_xT, g + 1)
                    if not (isinstance(g, int) and g == 0):
                        act.wait_ge(s_ln, g)
                    nc.scalar.activation(ee[:, 0, :], ps[:, p, :], ACT.Exp).then_inc(s_ex, 1)
                    act.wait_ge(s_ex, g + 1)
                    if not (isinstance(g, int) and g == 0):
                        act.wait_ge(s_xa, g)
                    nc.scalar.activation(te[:, 0, :], ee[:, 0, :], ACT.Ln, bias=1.0).then_inc(s_ln, 1)
                if mid:
                    m, pm = g - 1, (p + 1) % 2
                    act.wait_ge(s_J, m + 1)
                    if not (isinstance(m, int) and m == 0):
                        act.wait_ge(s_ln2, m)
                    nc.scalar.activation(ee[:, 1, :], ps[:, 2 + pm, :], ACT.Exp).then_inc(s_ex2, 1)
                    act.wait_ge(s_ex2, m + 1)
                    if not (isinstance(m, int) and m == 0):
                        act.wait_ge(s_xjf, m)
                    nc.scalar.activation(te[:, 1, :], ee[:, 1, :], ACT.Ln, bias=1.0).then_inc(s_ln2, 1)

            edges(act, step)

            act.wait_ge(s_bias, 1)
            nc.scalar.activation(expb[:, :], bias[:, :], ACT.Exp, scale=-1.0).then_inc(s_eb, 1)
            act.wait_ge(s_eb, 1)
            large = act.value_load(flag[0:1, 0:1], min_val=0, max_val=1)

            def softplus(i, s, q, short):
                n = PER * i + 2 * s + q
                lo = bank(s, q)
                biased = s not in (0, 2)
                again = s == 0 and not (isinstance(i, int) and i == 0)
                if again:
                    act.wait_ge(s_log, LN_PARTS * (n - 1))
                width = GROUP // EXP_PARTS
                for h in range(EXP_PARTS):
                    act.wait_ge(s_pe, 2 * n + (h + 1) * 2 // EXP_PARTS)
                    kw = {"bias": bias[:, s - 1:s]} if biased and not short else {}
                    nc.scalar.activation(e[:, q, h * width:(h + 1) * width],
                                         ps[:, lo:lo + 2, :].rearrange("p a b -> p (a b)")[:, h * width:(h + 1) * width],
                                         ACT.Exp, **kw).then_inc(s_exp, 1)
                one = expb[:, s - 1:s] if biased and short else 1.0
                if again:
                    act.wait_ge(s_u, 2 * (n - 1))
                width = GROUP // LN_PARTS
                for h in range(LN_PARTS):
                    act.wait_ge(s_exp, EXP_PARTS * n + -(-(h + 1) * EXP_PARTS // LN_PARTS))
                    nc.scalar.activation(t[:, q, h * width:(h + 1) * width], e[:, q, h * width:(h + 1) * width],
                                         ACT.Ln, bias=one).then_inc(s_log, 1)

            def all_pairs(short):
                def steps(i, first, end):
                    for s in range(first, end):
                        for q in range(2):
                            softplus(i, s, q, short)

                steps(0, 0, 1)
                with act.Fori(0, PAIRS - 1) as i:
                    steps(i, 1, STEPS)
                    steps(i + 1, 0, 1)
                steps(PAIRS - 1, 1, STEPS)

            with act.If(large == 0):
                all_pairs(short=True)
            with act.Else():
                all_pairs(short=False)

        @block.vector
        def _(dve):
            dve.wait_ge(s_w, NW)
            nc.vector.tensor_scalar(u1[:, :], u1[:, :], 1.0, None, ALU.add)
            dve.wait_ge(s_idx, 64)
            nc.vector.tensor_copy(src_f[:, :], src_i[:, :]).then_inc(s_cdve, 1)
            dve.wait_ge(s_const, 3)
            nc.vector.tensor_copy(dump_f[:, :], dump_i[:, 0:ET])
            dve.wait_ge(s_cdve, 1)
            nc.vector.tensor_tensor(out=diff_f[:, :], in0=src_f[:, :], in1=dump_i[:, :],
                                    op=ALU.subtract).then_inc(s_cdve, 1)
            dve.wait_ge(s_cdve, 2)
            nb = [0]

            def chained(instruction):
                instruction.then_inc(s_bv, 1)
                nb[0] += 1
                dve.wait_ge(s_bv, nb[0])

            dve.wait_ge(s_bps, 1)
            nc.vector.tensor_tensor(out=bj[:, :], in0=ps[0:1, 7, 384:512], in1=bj_raw[:, :], op=ALU.add)
            chained(nc.vector.tensor_tensor(out=bias[:, 0:1], in0=ps[:, 7, 0:1], in1=braw[:, 0:1], op=ALU.add))
            chained(nc.vector.scalar_tensor_tensor(out=bi_raw[:, :], in0=ps[:, 7, 128:256], scalar=-LN2,
                                                   in1=bi_raw[:, :], op0=ALU.add, op1=ALU.add))
            nc.vector.tensor_copy(zeros[:, :].rearrange("p (r f) -> p r f", f=F),
                                  bi_raw[:, :].unsqueeze(1).to_broadcast((128, ZROWS, F))).then_inc(s_zero, 1)
            chained(nc.vector.memset(bias[:, 1:2], 0.0))
            for l in range(NRES):
                for half, raw in ((0, 1 + l), (1, 1 + NRES + l)):
                    c = 1 + 2 * l + half
                    nc.vector.tensor_scalar(less[:, c:c + 1], bias[:, c:c + 1], -LN2, None, ALU.add).then_inc(s_less, 1)
                    dve.wait_ge(s_bps, 1 + c)
                    if half == 0:
                        chained(nc.vector.tensor_tensor(out=bias[:, c + 1:c + 2], in0=ps[:, 7, c:c + 1],
                                                        in1=braw[:, raw:raw + 1], op=ALU.add))
                    else:
                        chained(nc.vector.scalar_tensor_tensor(out=bias[:, c + 1:c + 2], in0=ps[:, 7, c:c + 1],
                                                               scalar=braw[:, raw:raw + 1], in1=bias[:, c - 1:c],
                                                               op0=ALU.add, op1=ALU.add))
            c = 1 + 2 * NRES
            chained(nc.vector.tensor_reduce(out=amax[:, :], in_=bias[:, :], axis=mybir.AxisListType.X, op=ALU.max,
                                            apply_absolute_value=True))
            nc.vector.tensor_scalar(dmat[:, :], negln2[:, :], bias[:, c:c + 1], None, ALU.add).then_inc(s_less, 1)
            dve.wait_ge(s_bps, 1 + c)
            nc.vector.tensor_tensor(out=bo[:, :], in0=ps[:, 7, 256:384], in1=bo_raw[:, :], op=ALU.add)
            chained(nc.vector.tensor_reduce(out=gmax[:, :], in_=ps[0:1, 7, 384:512], axis=mybir.AxisListType.X,
                                            op=ALU.max))
            nc.vector.tensor_scalar(flag[:, :], gmax[:, :], LIMIT, None, ALU.is_gt).then_inc(s_bias, 1)

            def step(k, p, front, mid, back):
                g = 2 * k + p
                if front:
                    dve.wait_ge(s_aT, g + 1)
                    nc.vector.tensor_copy(attrT[:, p, :], ps[0:K, 4, :]).then_inc(s_aTs, 1)
                    dve.wait_ge(s_ln, g + 1)
                    nc.vector.scalar_tensor_tensor(out=xaT[:, p, :], in0=te[:, 0, :], scalar=CAP,
                                                   in1=ps[:, p, :], op0=ALU.min, op1=ALU.max).then_inc(s_xa, 1)
                if mid:
                    m, pm = g - 1, (p + 1) % 2
                    km = (m - pm) // 2 if isinstance(m, int) else (k if pm == 0 else k - 1)
                    dve.wait_ge(s_la[pm], 32 * (km + 1))
                    targets = srow_tail[:, :] if isinstance(m, int) and m == EGROUPS - 1 else srow[:, pm, :]
                    for j in range(ET):
                        col = 4 * m + j
                        last = nc.vector.scalar_tensor_tensor(
                            out=same[:, pm, j, :, :],
                            in0=targets.rearrange("p (c j) -> p j c", j=ET),
                            scalar=src_f[:, bass.ds(col, 1)], in1=mask[:, j, :, :],
                            op0=ALU.is_equal, op1=ALU.mult, accum_out=cnt[:, pm, j:j + 1])
                    last.then_inc(s_same, 1)
                if back:
                    c = g - 2
                    dve.wait_ge(s_D, c + 1)
                    nc.vector.tensor_copy(comb[:, p, :], ps[:, 6, :]).then_inc(s_comb, 1)
                if mid:
                    dve.wait_ge(s_same, m + 1)
                    nc.vector.scalar_tensor_tensor(out=sel[:, :], in0=cnt[:, pm, :], scalar=1.0,
                                                   in1=diff_f[:, bass.ds(4 * m, ET)],
                                                   op0=ALU.is_equal, op1=ALU.mult).then_inc(s_sel, 1)
                    dve.wait_ge(s_ln2, m + 1)
                    nc.vector.scalar_tensor_tensor(out=xjf[:, :], in0=te[:, 1, :], scalar=CAP,
                                                   in1=ps[:, 2 + pm, :], op0=ALU.min,
                                                   op1=ALU.max).then_inc(s_xjf, 1)
                    dve.wait_ge(s_sel, m + 1)
                    if not (isinstance(m, int) and m < 2):
                        dve.wait_ge(s_sc, 16 * ET * (m - 1))
                    nc.vector.tensor_tensor(out=rows[:, pm, :], in0=sel[:, :], in1=dump_f[:, :],
                                            op=ALU.add).then_inc(s_rows, 1)
                    dve.wait_ge(s_xjf, m + 1)
                    dve.wait_ge(s_G, m + 1)
                    nc.vector.scalar_tensor_tensor(out=pxj[:, pm, :], in0=xjf[:, :], scalar=-LN2,
                                                   in1=ps[:, 5, :], op0=ALU.add,
                                                   op1=ALU.mult).then_inc(s_px, 1)

            edges(dve, step)
            dve.wait_ge(s_bias, 1)

            def softplus(i, s, q, short):
                n = PER * i + 2 * s + q
                lo = bank(s, q)
                if s == 0 and not (isinstance(i, int) and i == 0):
                    dve.wait_ge(s_o, 2 * (2 * (i - 1) + q) + 2)
                if short or s in (0, 2):
                    for h in range(2):
                        dve.wait_ge(s_log, LN_PARTS * n + (h * LN_PARTS) // 2 + 1)
                        half = slice(h * HALF, (h + 1) * HALF)
                        nc.vector.scalar_tensor_tensor(out=ug[:, q, half], in0=t[:, q, half], scalar=CAP,
                                                       in1=ps[:, lo + h, :], op0=ALU.min,
                                                       op1=ALU.max).then_inc(s_u, 1)
                    return
                nm = (PER - 4) * i + 2 * (s - 1 - (s > 2)) + q
                for h in range(2):
                    dve.wait_ge(s_log, LN_PARTS * n + (h * LN_PARTS) // 2 + 1)
                    half = slice(h * HALF, (h + 1) * HALF)
                    nc.vector.tensor_scalar(t[:, q, half], t[:, q, half], CAP, bias[:, s - 1:s], ALU.min,
                                            ALU.subtract).then_inc(s_min, 1)
                for h in range(2):
                    half = slice(h * HALF, (h + 1) * HALF)
                    dve.wait_ge(s_min, 2 * nm + h + 1)
                    nc.vector.tensor_tensor(out=ug[:, q, half], in0=ps[:, lo + h, :], in1=t[:, q, half],
                                            op=ALU.max).then_inc(s_u, 1)

            def add_x(i, q):
                n = 2 * i + q
                dve.wait_ge(s_xu, n + 1)
                for h in range(2):
                    dve.wait_ge(s_o, 2 * n + h + 1)
                    zh = z[:, q, 4 * h:4 * h + 4, :]
                    nc.vector.tensor_tensor(out=zh, in0=ps[:, 4 * q + h, :].rearrange("p (j f) -> p j f", f=F),
                                            in1=zh, op=ALU.add).then_inc(s_z, 1)

            def row_stats(i, q, h):
                n = 2 * i + q
                dve.wait_ge(s_z, 2 * n + h + 1)
                for j in range(4 * h, 4 * h + 4):
                    last = nc.vector.bn_stats(stats[:, q, j, :], z[:, q, j, :])
                if h:
                    last.then_inc(s_st, 1)

            def mean_variance(i, q):
                n = 2 * i + q
                dve.wait_ge(s_st, n + 1)
                dve.sem_inc(s_dpass, 1)
                for j in range(TILES):
                    last = nc.vector.bn_aggr(mv[:, q, j, :], stats[:, q, j, :])
                last.then_inc(s_mv, 1)

            def pair(i, short, first=False, last=False):
                for s in range(1, STEPS):
                    for q in range(2):
                        softplus(i, s, q, short)
                        if not first:
                            if s in (1, 2):
                                row_stats(i - 1, s - 1, q)
                            if s == 3:
                                mean_variance(i - 1, q)
                if not last:
                    for q in range(2):
                        softplus(i + 1, 0, q, short)
                        add_x(i, q)

            def all_pairs(short):
                for q in range(2):
                    softplus(0, 0, q, short)
                pair(0, short, first=True)
                with dve.Fori(1, PAIRS - 1) as i:
                    pair(i, short)
                pair(PAIRS - 1, short, last=True)

            large = dve.value_load(flag[0:1, 0:1], min_val=0, max_val=1)
            with dve.If(large == 0):
                all_pairs(short=True)
            with dve.Else():
                all_pairs(short=False)
            for q in range(2):
                add_x(PAIRS - 1, q)
            for q in range(2):
                row_stats(PAIRS - 1, q, 0)
                row_stats(PAIRS - 1, q, 1)
                mean_variance(PAIRS - 1, q)

        @block.tensor
        def _(pe):
            pe.wait_ge(s_w, NW)
            pe.wait_ge(s_const, 3)
            nc.tensor.matmul(ps[:, 7, 0:1], wi[:, :], negln2[:, 0:1], start=True, stop=True)
            nc.tensor.matmul(ps[:, 7, 128:256], negln2[:, :], wi[:, :], start=True, stop=True)
            nc.tensor.matmul(ps[:, 7, 384:512], negln2[:, :], wj[:, :], start=True, stop=True).then_inc(s_bps, 1)
            for c in range(1, 1 + 2 * NRES):
                pe.wait_ge(s_less, c)
                w = w1[:, (c - 1) // 2, :] if c % 2 else w2[:, (c - 1) // 2, :]
                nc.tensor.matmul(ps[:, 7, c:c + 1], w, less[:, c:c + 1], start=True, stop=True).then_inc(s_bps, 1)
            pe.wait_ge(s_less, 1 + 2 * NRES)
            nc.tensor.matmul(ps[:, 7, 256:384], dmat[:, :], wo[:, :], start=True, stop=True)
            nc.tensor.matmul(ps[0:1, 7, 384:512], amax[:, :], ident[:, :], start=True, stop=True).then_inc(s_bps, 1)
            pe.wait_ge(s_bias, 1)

            def step(k, p, front, mid, back):
                g = 2 * k + p
                if front:
                    pe.wait_ge(s_ga[p], 16 * ET * (k + 1))
                    pe.wait_ge(s_la[p], 32 * (k + 1))
                    if not (isinstance(g, int) and g == 0):
                        pe.wait_ge(s_aTs, g)
                    for j in range(ET):
                        last = nc.tensor.transpose(ps[:, p, j * 128:(j + 1) * 128], xe[:, p, j, :], ident[:, :])
                    last.then_inc(s_xT, 1)
                    for j in range(ET):
                        last = nc.tensor.transpose(ps[0:K, 4, j * 128:(j + 1) * 128], attr[:, p, j, :], ident[:, :])
                    last.then_inc(s_aT, 1)
                if back:
                    c = g - 2
                    pe.wait_ge(s_px, c + 1)
                    pe.wait_ge(s_same, c + 1)
                    if not (isinstance(c, int) and c == 0):
                        pe.wait_ge(s_comb, c)
                    for j in range(ET):
                        for jj in range(ET):
                            last = nc.tensor.matmul(ps[:, 6, j * F:(j + 1) * F], same[:, p, jj, j, :],
                                                    pxj[:, p, jj * F:(jj + 1) * F],
                                                    start=(jj == 0), stop=(jj == ET - 1))
                    last.then_inc(s_D, 1)
                if mid:
                    m, pm = g - 1, (p + 1) % 2
                    pe.wait_ge(s_xa, m + 1)
                    for j in range(ET):
                        o = ps[:, 2 + pm, j * F:(j + 1) * F]
                        nc.tensor.matmul(o, xaT[:, pm, j * 128:(j + 1) * 128], wj[:, :], start=True, stop=False)
                        last = nc.tensor.matmul(o, ones_row[:, :], bj[:, :], start=False, stop=True)
                    last.then_inc(s_J, 1)
                    pe.wait_ge(s_aTs, m + 1)
                    for j in range(ET):
                        last = nc.tensor.matmul(ps[:, 5, j * F:(j + 1) * F], attrT[:, pm, j * 128:(j + 1) * 128],
                                                wk[:, :], start=True, stop=True)
                    last.then_inc(s_G, 1)

            edges(pe, step)
            pe.wait_ge(s_comb, EGROUPS)

            def layer(i, s, q):
                n = PER * i + 2 * s + q
                lo = bank(s, q)
                if s == 0:
                    pe.wait_ge(s_x[q], 16 * (i + 1))
                    if not (isinstance(i, int) and i == 0):
                        pe.wait_ge(s_u, 2 * (n - 4) + 2)
                    for h in range(2):
                        for j in range(4):
                            last = nc.tensor.transpose(ps[:, lo + h, j * 128:(j + 1) * 128],
                                                       x_nat[:, q, 4 * h + j, :], ident[:, :])
                        last.then_inc(s_pe, 1)
                    return
                if s == 2:
                    if not (isinstance(i, int) and i == 0):
                        pe.wait_ge(s_z, 2 * (2 * (i - 1) + q) + 2)
                    pe.wait_ge(s_xj[q], 16 * (i + 1))
                    for h in range(2):
                        for j in range(4):
                            nc.tensor.matmul(ps[:, lo + h, j * 128:(j + 1) * 128], xj_nat[:, q, 4 * h + j, :],
                                             ident[:, :], is_transpose=True, start=(j == 0), stop=True,
                                             skip_group_check=True)
                w = (wi[:, :] if s == 1 else ident[:, :] if s == 2 else
                     w1[:, (s - 3) // 2, :] if s % 2 else w2[:, (s - 4) // 2, :])
                for h in range(2):
                    pe.wait_ge(s_u, 2 * (n - 2) + h + 1)
                    nc.tensor.matmul(ps[:, lo + h, :], w, ug[:, q, h * HALF:(h + 1) * HALF],
                                     start=bool(s % 2), stop=True,
                                     skip_group_check=not s % 2).then_inc(s_pe, 1)

            def output(i, q):
                n = PER * i + 2 * (STEPS - 1) + q
                for h in range(2):
                    pe.wait_ge(s_u, 2 * n + h + 1)
                    for j in range(4):
                        c = 4 * h + j
                        last = nc.tensor.matmul(ps[:, 4 * q + h, j * F:(j + 1) * F],
                                                ug[:, q, c * 128:(c + 1) * 128], wo[:, :], start=True, stop=True)
                    last.then_inc(s_o, 1)

            def pair(i, last=False):
                for s in range(1, STEPS):
                    for q in range(2):
                        layer(i, s, q)
                if not last:
                    for q in range(2):
                        layer(i + 1, 0, q)
                for q in range(2):
                    output(i, q)

            for q in range(2):
                layer(0, 0, q)
            pair(0)
            with pe.Fori(1, PAIRS - 1) as i:
                pair(i)
            pair(PAIRS - 1, last=True)


_INS = ['x', 'src', 'dst', 'edge_attr_64', 'L0_gnn_W_k2f', 'L0_gnn_W_i', 'L0_gnn_b_i', 'L0_gnn_W_j', 'L0_gnn_b_j',
        'L0_gnn_W_res1', 'L0_gnn_b_res1', 'L0_gnn_W_res2', 'L0_gnn_b_res2', 'L0_gnn_W_out', 'L0_gnn_b_out',
        'L0_gnn_u']


def kernel(**inputs):
    import numpy as _np
    import concourse.bacc as _bacc
    from concourse import mybir as _mybir
    from concourse.bass_utils import run_bass_kernel_spmd as _run

    nc = _bacc.Bacc("TRN2", target_bir_lowering=False, num_devices=1)
    arrays, args = {}, []
    for name in _INS:
        a = _np.ascontiguousarray(inputs[name])
        arrays[f"in_{name}_dram"] = a
        args.append(nc.dram_tensor(f"in_{name}_dram", a.shape, _mybir.dt.from_np(a.dtype), kind="ExternalInput").ap())
    shape = inputs['x'].shape
    args.append(nc.dram_tensor("out_0_dram", shape, _mybir.dt.float32, kind="ExternalOutput").ap())
    gnn_kernel(nc, *args)
    r = _run(nc, [arrays], core_ids=[0])
    return r.results[0]["out_0_dram"]
```

```python
import math

import concourse.bass as bass
from concourse import mybir
from contextlib import ExitStack

F = 128
LN2 = math.log(2.0)
CAP = 40.0
LIMIT = 16.0
EPS = 1e-5


def gnn_kernel(nc, x, src, dst, edge_attr, w_k2f, w_i, b_i, w_j, b_j, w_res1, b_res1, w_res2, b_res2,
               w_out, b_out, u, out):
    fp32 = mybir.dt.float32
    bf16 = mybir.dt.bfloat16
    i32 = mybir.dt.int32
    u32 = mybir.dt.uint32
    ALU = mybir.AluOpType
    ACT = mybir.ActivationFunctionType

    N = x.shape[0]
    E, K = edge_attr.shape
    NRES = w_res1.shape[0]

    GROUP = 1024
    TILES = GROUP // 128
    HALF = 512
    PAIR = 2 * GROUP
    PAIRS = -(-N // PAIR)
    LAST = N - PAIR
    STEPS = 3 + 2 * NRES
    PER = 2 * (STEPS - 2)
    UNITS = PAIR // HALF

    EG = 512
    ET = EG // 128
    EGROUPS = -(-E // EG)
    TAIL = E - (EGROUPS - 1) * EG
    TAILT, TAILP = TAIL // 128, TAIL % 128
    ITILES = -(-E // 128)
    assert TAILP > 0 and 128 < ITILES <= 256 and EGROUPS % 2 == 1 and EGROUPS == PAIRS
    DUMP = N + 1
    CROWS = 22
    CCHUNKS = -(-(DUMP + EG) // (128 * CROWS))
    ACC_ROWS = 128 * CROWS * CCHUNKS

    acc = nc.dram_tensor("message_sums", (ACC_ROWS, F), fp32, kind="Internal").ap()
    xi_dram = nc.dram_tensor("atom_layer_results", (PAIRS * PAIR, F), fp32, kind="Internal").ap()
    acc_chunks = acc.rearrange("(p r) f -> p (r f)", p=128)

    ctx = ExitStack()
    with ctx:
        def sb(name, shape, dt=fp32):
            return ctx.enter_context(nc.sbuf_tensor(name, shape, dt))

        def sem(name):
            return ctx.enter_context(nc.semaphore(name))

        ident = sb("ident", [128, 128])
        negln2 = sb("negln2", [128, 128])
        ones = sb("ones", [128, 128], bf16)
        brow = sb("brow", [128, 3, F])
        rest = sb("rest", [128, 2, F])
        part = sb("part", [128, 2, F], bf16)
        brows = sb("brows", [128, 2, 4, F], bf16)
        w1 = sb("w1", [128, NRES, F])
        w2 = sb("w2", [128, NRES, F])
        wi = sb("wi", [128, F])
        wj = sb("wj", [128, F])
        wo = sb("wo", [128, F])
        wk = sb("wk", [2 * K, 2, F])
        braw = sb("braw", [128, 2 * NRES])
        bias = sb("bias", [128, 1 + 2 * NRES])
        less = sb("less", [128, 1 + 2 * NRES])
        expb = sb("expb", [128, 1 + 2 * NRES])
        dmat = sb("dmat", [128, 128])
        amax = sb("amax", [128, 1])
        gmax = sb("gmax", [1, 1])
        flag = sb("flag", [1, 1], i32)
        u1 = sb("u1", [128, F])
        start_rows = sb("start_rows", [128, CROWS * F])
        irow = sb("irow", [128, 2, 2, 128], i32)
        irow_f = sb("irow_f", [128, 2, 2, 128])
        dst_i = sb("dst_i", [128, 256], i32)
        src_f = sb("src_f", [128, 256])
        dump_i = sb("dump_i", [128, EGROUPS * ET], i32)
        dump_f = sb("dump_f", [128, ET])
        diff_f = sb("diff_f", [128, EGROUPS * ET])
        mask = sb("mask", [128, EG])
        dst_now = sb("dst_now", [128, 2, ET], i32)
        xe = sb("xe", [128, 2, ET, F])
        attr = sb("attr", [128, 2, ET, K])
        srow = sb("srow", [128, 2, EG], i32)
        srow_tail = sb("srow_tail", [128, EG], i32)
        ee = sb("ee", [128, 2, EG])
        te = sb("te", [128, 2, EG])
        xaT = sb("xaT", [128, 2, EG])
        attrT = sb("attrT", [2 * K, EG // 2])
        xjf = sb("xjf", [128, EG])
        pxj = sb("pxj", [128, 2, EG])
        same = sb("same", [128, 2, ET, EG])
        cnt = sb("cnt", [128, 2, ET])
        sel = sb("sel", [128, ET])
        rows = sb("rows", [128, 2, ET], u32)
        comb = sb("comb", [128, 2, EG])
        x_nat = sb("x_nat", [128, 2, TILES, F])
        xj_nat = sb("xj_nat", [128, 2, TILES, F])
        xi_nat = sb("xi_nat", [128, 2, TILES, F])
        z = sb("z", [128, 2, TILES, F])
        e = sb("e", [128, 2, GROUP])
        t = sb("t", [128, 2, GROUP])
        ug = sb("ug", [128, 2, GROUP])
        uf = sb("uf", [128, 2, GROUP])
        stats = sb("stats", [128, 2, TILES, 6])
        mv = sb("mv", [128, 2, TILES, 2])
        veps = sb("veps", [128, 2, TILES])
        minus_half = sb("minus_half", [128, TILES])
        minus_one = sb("minus_one", [128, TILES])
        eps_row = sb("eps_row", [128, TILES])
        rstd = sb("rstd", [128, 2, TILES])
        shift = sb("shift", [128, 2, TILES])

        ps = ctx.enter_context(nc.psum_tensor("ps", [128, 8, 512], fp32))

        s_w = sem("weights_loaded")
        s_idx = sem("indices_loaded")
        s_pad = sem("padding_set")
        s_const = sem("constants_made")
        s_iT = sem("indices_transposed")
        s_cdve = sem("constants_dve")
        s_bps = sem("bias_sums_ready")
        s_less = sem("bias_inputs_ready")
        s_bv = sem("bias_chain")
        s_bias = sem("biases_ready")
        s_eb = sem("exp_bias_ready")
        s_start = sem("start_rows_ready")
        s_filled = sem("table_filled")
        s_ga = [sem("gathered_even"), sem("gathered_odd")]
        s_la = [sem("edge_loads_even"), sem("edge_loads_odd")]
        s_pass = sem("pool_passed")
        s_dpass = sem("vector_passed")
        s_now = sem("gather_indices_ready")
        s_xT = sem("edge_xT")
        s_aT = sem("edge_attrT")
        s_aTs = sem("edge_attrT_sbuf")
        s_ex = sem("edge_exp")
        s_ln = sem("edge_ln")
        s_xa = sem("edge_xa_ready")
        s_J = sem("edge_J_ready")
        s_G = sem("edge_G_ready")
        s_ex2 = sem("edge_exp2")
        s_ln2 = sem("edge_ln2")
        s_xjf = sem("edge_xjf")
        s_px = sem("edge_pxj_ready")
        s_same = sem("edge_same_ready")
        s_sel = sem("edge_sel")
        s_rows = sem("edge_rows_ready")
        s_D = sem("edge_D_ready")
        s_comb = sem("edge_comb_ready")
        s_sc = sem("scattered")

        s_X = sem("x_transposed")
        s_XE = sem("x_exp_ready")
        s_XL = sem("x_log_ready")
        s_XU = sem("xa_ready")
        s_P = sem("xi_product_ready")
        s_PE = sem("xi_exp_ready")
        s_PL = sem("xi_log_ready")
        s_PU = sem("xi_ready")
        s_sp = [sem("xi_stored_A"), sem("xi_stored_B")]

        s_x = [sem("x_loaded_A"), sem("x_loaded_B")]
        s_xi = [sem("xi_loaded_A"), sem("xi_loaded_B")]
        s_add = sem("sum_ready")
        s_xj = [sem("xj_loaded_A"), sem("xj_loaded_B")]
        s_pe = sem("product_ready")
        s_exp = sem("exp_ready")
        s_log = sem("log_ready")
        s_min = sem("capped")
        s_u = sem("softplus_ready")
        s_o = sem("output_product_ready")
        s_z = sem("z_ready")
        s_st = sem("stats_ready")
        s_mv = sem("mean_var_ready")
        s_xm = sem("x_times_u")
        s_xu = sem("x_part_ready")
        s_ve = sem("var_eps")
        s_rs = sem("rstd_ready")
        s_nm = sem("shift_ready")
        s_norm = sem("normalised")
        s_out = [sem("stored_A"), sem("stored_B")]

        block = ctx.enter_context(nc.Block())

        NW = 13 * 16


        def bank(s, q):
            return 4 * q + 2 * (s % 2)

        def edges(engine, step):
            step(0, 0, True, False, False)
            step(0, 1, True, True, False)
            with engine.Fori(1, EGROUPS // 2) as k:
                step(k, 0, True, True, True)
                step(k, 1, True, True, True)
            k = EGROUPS // 2
            step(k, 0, True, True, True)
            step(k, 1, False, True, True)
            step(k + 1, 0, False, False, True)

        @block.sync
        def _(sp):
            full = (EGROUPS - 1) * EG
            sp.wait_ge(s_pad, 1)
            for c, dram in enumerate((dst, src)):
                sp.dma_start(irow[:, c, 0, :], dram[0:128 * 128].rearrange("(p e) -> p e", e=128)).then_inc(s_idx, 16)
                sp.dma_start(irow[0:ITILES - 129, c, 1, :],
                             dram[128 * 128:(ITILES - 1) * 128].rearrange("(p e) -> p e", e=128)).then_inc(s_idx, 16)
                sp.dma_start(irow[ITILES - 129:ITILES - 128, c, 1, 0:TAILP],
                             dram[(ITILES - 1) * 128:E].rearrange("(o e) -> o e", o=1)).then_inc(s_idx, 16)

            def load_edges(g, k, p, tail=False):
                if not tail:
                    sp.dma_start(attr[:, p, :, :],
                                 edge_attr[bass.ds(g * EG, EG), :].rearrange("(j p) c -> p j c", j=ET)
                                 ).then_inc(s_la[p], 16)
                    sp.dma_start(srow[:, p, :],
                                 src[bass.ds(g * EG, EG)].rearrange("(o e) -> o e", o=1)
                                 .to_broadcast((128, EG))).then_inc(s_la[p], 16)
                else:
                    sp.dma_start(attr[:, p, 0:TAILT, :], edge_attr[full:full + TAILT * 128, :]
                                 .rearrange("(j p) c -> p j c", p=128)).then_inc(s_la[p], 16)
                    sp.dma_start(attr[0:TAILP, p, TAILT, :], edge_attr[full + TAILT * 128:E, :]).then_inc(s_la[p], 16)
                    sp.dma_start(srow_tail[:, 0:TAIL],
                                 src[full:E].rearrange("(o e) -> o e", o=1)
                                 .to_broadcast((128, TAIL))).then_inc(s_la[p], 16)

            def load_x(base, q):
                sp.dma_start(x_nat[:, q, :, :], x[bass.ds(base + q * GROUP, GROUP), :]
                             .rearrange("(p j) f -> p j f", j=TILES)).then_inc(s_x[q], 16)

            load_edges(0, 0, 0)
            load_x(0, 0)
            load_x(0, 1)
            load_edges(1, 0, 1)
            sp.dma_start(wi[:, :], w_i).then_inc(s_w, 16)
            sp.dma_start(wj[:, :], w_j).then_inc(s_w, 16)
            sp.dma_start(wo[:, :], w_out).then_inc(s_w, 16)
            sp.dma_start(wk[0:K, 0, :], w_k2f).then_inc(s_w, 16)
            sp.dma_start(wk[K:2 * K, 1, :], w_k2f).then_inc(s_w, 16)
            sp.dma_start(w1[:, :, :], w_res1.rearrange("l k f -> k l f")).then_inc(s_w, 16)
            sp.dma_start(w2[:, :, :], w_res2.rearrange("l k f -> k l f")).then_inc(s_w, 16)
            with nc.allow_non_contiguous_dma(reason="bias columns, once"):
                sp.dma_start(braw[:, 0:NRES], b_res1.rearrange("l f -> f l")).then_inc(s_w, 16)
                sp.dma_start(braw[:, NRES:2 * NRES], b_res2.rearrange("l f -> f l")).then_inc(s_w, 16)
            for c, b in enumerate((b_i, b_j, b_out)):
                sp.dma_start(brow[:, c, :], b.rearrange("(o f) -> o f", o=1).to_broadcast((128, F))).then_inc(s_w, 16)
            sp.dma_start(u1[:, :], u.rearrange("(o f) -> o f", o=1).to_broadcast((128, F))).then_inc(s_w, 16)

            def load_xj(base, q):
                sp.dma_start(xj_nat[:, q, :, :], acc[bass.ds(base + q * GROUP, GROUP), :]
                             .rearrange("(p j) f -> p j f", j=TILES)).then_inc(s_xj[q], 16)

            def load_xi(i, q):
                sp.dma_start(xi_nat[:, q, :, :], xi_dram[bass.ds(i * PAIR + q * GROUP, GROUP), :]
                             .rearrange("(p j) f -> p j f", j=TILES)).then_inc(s_xi[q], 16)

            def store_xi(i, q):
                sp.wait_ge(s_PU, UNITS * i + 2 * q + 2)
                sp.dma_start(xi_dram[bass.ds(i * PAIR + q * GROUP, GROUP), :]
                             .rearrange("(p j) f -> p j f", j=TILES), z[:, q, :, :]).then_inc(s_sp[q], 16)

            def fill_table(first, end):
                with sp.Fori(first, end) as c:
                    sp.dma_start(acc_chunks[:, bass.ds(c * (CROWS * F), CROWS * F)], start_rows[:, :]).then_inc(s_filled, 16)

            def next_x(i, base, q):
                sp.wait_ge(s_X, UNITS * (i - 1) + 2 * q + 2)
                load_x(base, q)

            def next_edges(g, p, tail=False):
                sp.wait_ge(s_aT, g - 1)
                sp.wait_ge(s_same, g - 1)
                load_edges(g, None, p, tail)

            def around(g, p, base, tail=False):
                next_x(g, base, 0)
                if not (isinstance(g, int) and g < 2):
                    store_xi(g - 2, 1)
                next_x(g, base, 1)
                store_xi(g - 1, 0)
                if not (isinstance(g, int) and g < 2):
                    next_edges(g, p, tail)

            sp.wait_ge(s_start, 1)
            for c in range(3):
                fill_table(c * CCHUNKS // 3, (c + 1) * CCHUNKS // 3)
                around(c + 1, (c + 1) % 2, (c + 1) * PAIR)

            with sp.Fori(2, EGROUPS // 2) as k:
                for p in range(2):
                    around(2 * k + p, p, (2 * k + p) * PAIR)
            g = EGROUPS - 1
            around(g, 0, LAST, tail=True)
            store_xi(g - 1, 1)
            store_xi(g, 0)
            store_xi(g, 1)

            for q in range(2):
                sp.wait_ge(s_X, UNITS * PAIRS)
                load_x(0, q)
                sp.wait_ge(s_sp[q], 16 * PAIRS)
                load_xi(0, q)
            sp.wait_ge(s_sc, EGROUPS * ET * 16)
            load_xj(0, 0)
            load_xj(0, 1)

            def store(i, base, q):
                sp.wait_ge(s_norm, 2 * i + q + 1)
                sp.dma_start(out[bass.ds(base + q * GROUP, GROUP), :].rearrange("(p j) f -> p j f", j=TILES),
                             z[:, q, :, :]).then_inc(s_out[q], 16)

            def pair(i, base, base_next, base_before):
                for q in range(2):
                    sp.wait_ge(s_pe, 2 * (PER * i + q) + 2)
                    load_xj(base_next, q)
                    load_xi(i + 1, q)
                if base_before is not None:
                    for q in range(2):
                        sp.wait_ge(s_z, 2 * (2 * (i - 1) + q) + 2)
                        load_x(base, q)
                if base_before is not None:
                    store(i - 1, base_before, 0)
                    store(i - 1, base_before, 1)

            pair(0, 0, PAIR, None)
            with sp.Fori(1, PAIRS - 2) as i:
                pair(i, i * PAIR, (i + 1) * PAIR, (i - 1) * PAIR)
            pair(PAIRS - 2, (PAIRS - 2) * PAIR, LAST, (PAIRS - 3) * PAIR)
            i = PAIRS - 1
            for q in range(2):
                sp.wait_ge(s_z, 2 * (2 * (i - 1) + q) + 2)
                load_x(LAST, q)
            store(i - 1, (i - 1) * PAIR, 0)
            store(i - 1, (i - 1) * PAIR, 1)
            sp.wait_ge(s_out[0], 16 * i)
            sp.wait_ge(s_out[1], 16 * i)
            store(i, LAST, 0)
            store(i, LAST, 1)
            sp.wait_ge(s_out[0], 16 * PAIRS)
            sp.wait_ge(s_out[1], 16 * PAIRS)

        @block.gpsimd
        def _(pool):
            nc.gpsimd.memset(irow[:, 0, 1, :], 0)
            nc.gpsimd.memset(srow_tail[:, :], N)
            nc.gpsimd.memset(wk[:, :, :], 0.0)
            nc.gpsimd.memset(irow[:, 1, 1, :], N).then_inc(s_pad, 1)
            nc.gpsimd.memset(start_rows[:, :], -LN2).then_inc(s_start, 1)
            nc.gpsimd.memset(ident[:, :], 0.0).then_inc(s_const, 1)
            nc.gpsimd.memset(brows[:, :, :, :], 0.0)
            nc.gpsimd.memset(ones[:, :], 1.0)
            nc.gpsimd.memset(negln2[:, :], -LN2)
            nc.gpsimd.memset(minus_half[:, :], -0.5)
            nc.gpsimd.memset(minus_one[:, :], -1.0)
            nc.gpsimd.memset(eps_row[:, :], EPS)
            nc.gpsimd.memset(mask[:, :], 1.0).then_inc(s_const, 1)
            nc.gpsimd.iota(dump_i[:, :].rearrange("p (g j) -> p g j", j=ET), pattern=[[0, EGROUPS], [128, ET]],
                           base=DUMP, channel_multiplier=1)
            pool.wait_ge(s_const, 1)
            nc.gpsimd.affine_select(out=ident[:, :], in_=ident[:, :], compare_op=ALU.not_equal, fill=1.0, base=0,
                                    pattern=[[-1, 128]], channel_multiplier=1)
            pool.wait_ge(s_const, 2)
            nc.gpsimd.affine_select(out=mask[:, EG - 128:EG], in_=mask[:, EG - 128:EG], compare_op=ALU.is_ge,
                                    fill=0.0, base=0, pattern=[[-1, 128]], channel_multiplier=1).then_inc(s_const, 1)
            pool.wait_ge(s_cdve, 2)

            def gather(g, p):
                nc.gpsimd.tensor_copy(dst_now[:, p, :], dst_i[:, bass.ds(g * ET, ET)]).then_inc(s_now, 1)
                pool.wait_ge(s_now, g + 1)
                pool.sem_inc(s_pass, 1)
                for j in range(ET):
                    nc.gpsimd.indirect_dma_start(
                        out=xe[:, p, j, :], out_offset=None, in_=x,
                        in_offset=bass.IndirectOffsetOnAxis(ap=dst_now[:, p, j:j + 1], axis=0)
                    ).then_inc(s_ga[p], 16)

            gather(0, 0)

            def step(k, p, front, mid, back):
                g = 2 * k + p
                if front and not (isinstance(k, int) and k == EGROUPS // 2):
                    if not (isinstance(g, int) and g == 0):
                        pool.wait_ge(s_xT, g)
                    gather(g + 1, (p + 1) % 2)
                if back:
                    c = g - 2
                    pool.wait_ge(s_filled, 16 * CCHUNKS)
                    pool.wait_ge(s_comb, c + 1)
                    if not (isinstance(c, int) and c == 0):
                        pool.wait_ge(s_sc, 16 * ET * c)
                    pool.sem_inc(s_pass, 1)
                    for j in range(ET):
                        nc.gpsimd.indirect_dma_start(
                            out=acc, out_offset=bass.IndirectOffsetOnAxis(ap=rows[:, p, j:j + 1], axis=0),
                            in_=comb[:, p, j * F:(j + 1) * F], in_offset=None,
                            compute_op=ALU.add).then_inc(s_sc, 16)

            edges(pool, step)

            def times_u(i, q):
                pool.wait_ge(s_x[q], 16 * (PAIRS + i + 1))
                nc.gpsimd.tensor_tensor(out=x_nat[:, q, :, :], in0=x_nat[:, q, :, :],
                                        in1=u1[:, :].unsqueeze(1).to_broadcast((128, TILES, F)),
                                        op=ALU.mult).then_inc(s_xm, 1)

            def add_bias(i, q):
                pool.wait_ge(s_xm, 2 * i + q + 1)
                nc.gpsimd.tensor_tensor(out=x_nat[:, q, :, :], in0=x_nat[:, q, :, :],
                                        in1=brow[:, 2, :].unsqueeze(1).to_broadcast((128, TILES, F)),
                                        op=ALU.add).then_inc(s_xu, 1)

            def add_sums(i, q):
                pool.wait_ge(s_xj[q], 16 * (i + 1))
                pool.wait_ge(s_xi[q], 16 * (i + 1))
                nc.gpsimd.tensor_tensor(out=xj_nat[:, q, :, :], in0=xj_nat[:, q, :, :], in1=xi_nat[:, q, :, :],
                                        op=ALU.add).then_inc(s_add, 1)

            def normalise(i, q):
                n = 2 * i + q + 1
                pool.wait_ge(s_const, 3)
                pool.wait_ge(s_mv, n)
                nc.gpsimd.tensor_tensor(out=veps[:, q, :], in0=mv[:, q, :, 1], in1=eps_row[:, :],
                                        op=ALU.add).then_inc(s_ve, 1)
                pool.wait_ge(s_ve, n)
                nc.gpsimd.tensor_tensor(out=rstd[:, q, :], in0=veps[:, q, :], in1=minus_half[:, :],
                                        op=ALU.pow).then_inc(s_rs, 1)
                pool.wait_ge(s_rs, n)
                nc.gpsimd.tensor_tensor(out=shift[:, q, :], in0=mv[:, q, :, 0], in1=rstd[:, q, :],
                                        op=ALU.mult).then_inc(s_nm, 1)
                pool.wait_ge(s_nm, 2 * n - 1)
                nc.gpsimd.tensor_tensor(out=shift[:, q, :], in0=shift[:, q, :], in1=minus_one[:, :],
                                        op=ALU.mult).then_inc(s_nm, 1)
                pool.wait_ge(s_nm, 2 * n)
                pool.sem_inc(s_pass, 1)
                for j in range(TILES):
                    last = nc.gpsimd.tensor_scalar(z[:, q, j, :], z[:, q, j, :], rstd[:, q, j:j + 1],
                                                   shift[:, q, j:j + 1], ALU.mult, ALU.add)
                last.then_inc(s_norm, 1)

            pool.wait_ge(s_bias, 1)
            for i in range(2):
                for q in range(2):
                    add_sums(i, q)
                if i == 0:
                    for q in range(2):
                        times_u(0, q)
                    for q in range(2):
                        add_bias(0, q)

            def pair(i, last=False):
                if not last:
                    for q in range(2):
                        add_sums(i + 1, q)
                for q in range(2):
                    times_u(i, q)
                for q in range(2):
                    normalise(i - 1, q)
                for q in range(2):
                    add_bias(i, q)

            with pool.Fori(1, PAIRS - 1) as i:
                pair(i)
            pair(PAIRS - 1, last=True)
            for q in range(2):
                normalise(PAIRS - 1, q)

        @block.scalar
        def _(act):
            nc.scalar.preload_act_table_set("natural_log_exp_and_others")

            def atoms0_exp(g, u):
                v, b = UNITS * g + u, u % 2
                act.wait_ge(s_X, v + 1)
                if not (isinstance(g, int) and g == 0 and u < 2):
                    act.wait_ge(s_XL, v - 1)
                nc.scalar.activation(e[:, 0, b * HALF:(b + 1) * HALF], ps[:, 4 + b, :], ACT.Exp).then_inc(s_XE, 1)

            def atoms0_ln(g, u):
                v, b = UNITS * g + u, u % 2
                act.wait_ge(s_XE, v + 1)
                if not (isinstance(g, int) and g == 0 and u < 2):
                    act.wait_ge(s_XU, v - 1)
                nc.scalar.activation(t[:, 0, b * HALF:(b + 1) * HALF], e[:, 0, b * HALF:(b + 1) * HALF], ACT.Ln,
                                     bias=1.0).then_inc(s_XL, 1)

            def atoms1_exp(g, u):
                v, b = UNITS * g + u - 2, u % 2
                act.wait_ge(s_P, v + 1)
                if not (isinstance(v, int) and v < 2):
                    act.wait_ge(s_PL, v - 1)
                nc.scalar.activation(e[:, 1, b * HALF:(b + 1) * HALF], ps[:, 6 + b, :], ACT.Exp).then_inc(s_PE, 1)

            def atoms1_ln(g, u):
                v, b = UNITS * g + u - 2, u % 2
                act.wait_ge(s_PE, v + 1)
                if not (isinstance(v, int) and v < 2):
                    act.wait_ge(s_PU, v - 1)
                nc.scalar.activation(t[:, 1, b * HALF:(b + 1) * HALF], e[:, 1, b * HALF:(b + 1) * HALF], ACT.Ln,
                                     bias=1.0).then_inc(s_PL, 1)

            def edge_x_exp(g, p):
                act.wait_ge(s_xT, g + 1)
                if not (isinstance(g, int) and g == 0):
                    act.wait_ge(s_ln, g)
                nc.scalar.activation(ee[:, 0, :], ps[:, p, :], ACT.Exp).then_inc(s_ex, 1)

            def edge_x_ln(g):
                act.wait_ge(s_ex, g + 1)
                if not (isinstance(g, int) and g == 0):
                    act.wait_ge(s_xa, g)
                nc.scalar.activation(te[:, 0, :], ee[:, 0, :], ACT.Ln, bias=1.0).then_inc(s_ln, 1)

            def edge_j_exp(m, pm):
                act.wait_ge(s_J, m + 1)
                if not (isinstance(m, int) and m == 0):
                    act.wait_ge(s_ln2, m)
                nc.scalar.activation(ee[:, 1, :], ps[:, pm, :], ACT.Exp).then_inc(s_ex2, 1)

            def edge_j_ln(m):
                act.wait_ge(s_ex2, m + 1)
                if not (isinstance(m, int) and m == 0):
                    act.wait_ge(s_xjf, m)
                nc.scalar.activation(te[:, 1, :], ee[:, 1, :], ACT.Ln, bias=1.0).then_inc(s_ln2, 1)

            def step(k, p, front, mid, back):
                g = 2 * k + p
                for u in range(UNITS):
                    step1 = (front or u < 2 and mid) and not (isinstance(g, int) and g == 0 and u < 2)
                    if step1:
                        atoms1_exp(g, u)
                    if front:
                        atoms0_exp(g, u)
                    if step1:
                        atoms1_ln(g, u)
                    if front:
                        atoms0_ln(g, u)
                    if mid and u == 0:
                        edge_j_exp(g - 1, (p + 1) % 2)
                    if front and u == 1:
                        edge_x_exp(g, p)
                    if front and u == 2:
                        edge_x_ln(g)
                    if mid and u == 3:
                        edge_j_ln(g - 1)

            edges(act, step)

            act.wait_ge(s_bias, 1)
            nc.scalar.activation(expb[:, :], bias[:, :], ACT.Exp, scale=-1.0).then_inc(s_eb, 1)
            act.wait_ge(s_eb, 1)
            large = act.value_load(flag[0:1, 0:1], min_val=0, max_val=1)

            def softplus(i, s, q, short):
                n = PER * i + 2 * (s - 2) + q
                lo = bank(s, q)
                for h in range(2):
                    act.wait_ge(s_pe, 2 * n + h + 1)
                    kw = {"bias": bias[:, s - 2:s - 1]} if s > 2 and not short else {}
                    nc.scalar.activation(e[:, q, h * HALF:(h + 1) * HALF], ps[:, lo + h, :], ACT.Exp,
                                         **kw).then_inc(s_exp, 1)
                one = expb[:, s - 2:s - 1] if s > 2 and short else 1.0
                for h in range(2):
                    act.wait_ge(s_exp, 2 * n + h + 1)
                    nc.scalar.activation(t[:, q, h * HALF:(h + 1) * HALF], e[:, q, h * HALF:(h + 1) * HALF],
                                         ACT.Ln, bias=one).then_inc(s_log, 1)

            def all_pairs(short):
                with act.Fori(0, PAIRS) as i:
                    for s in range(2, STEPS):
                        for q in range(2):
                            softplus(i, s, q, short)

            with act.If(large == 0):
                all_pairs(short=True)
            with act.Else():
                all_pairs(short=False)

        @block.vector
        def _(dve):
            dve.wait_ge(s_idx, 96)
            nc.vector.tensor_copy(irow_f[:, :, :, :], irow[:, :, :, :]).then_inc(s_cdve, 1)
            dve.wait_ge(s_iT, 1)
            nc.vector.tensor_copy(dst_i[:, :], ps[:, 0, 0:256]).then_inc(s_cdve, 1)
            nc.vector.tensor_copy(src_f[:, :], ps[:, 1, 0:256]).then_inc(s_cdve, 1)
            dve.wait_ge(s_const, 3)
            nc.vector.tensor_copy(dump_f[:, :], dump_i[:, 0:ET])
            dve.wait_ge(s_cdve, 3)
            nc.vector.tensor_tensor(out=diff_f[:, :], in0=src_f[:, 0:EGROUPS * ET], in1=dump_i[:, :],
                                    op=ALU.subtract).then_inc(s_cdve, 1)
            dve.wait_ge(s_w, NW)
            nc.vector.tensor_scalar(u1[:, :], u1[:, :], 1.0, None, ALU.add)
            dve.wait_ge(s_cdve, 4)
            nb = [0]

            def chained(instruction):
                instruction.then_inc(s_bv, 1)
                nb[0] += 1
                dve.wait_ge(s_bv, nb[0])

            dve.wait_ge(s_bps, 1)
            nc.vector.tensor_tensor(out=brow[:, 0, :], in0=ps[:, 7, 128:256], in1=brow[:, 0, :], op=ALU.add)
            chained(nc.vector.tensor_tensor(out=brow[:, 1, :], in0=ps[:, 7, 384:512], in1=brow[:, 1, :], op=ALU.add))

            value = brow
            for a in range(3):
                chained(nc.vector.tensor_copy(part[:, :, :], value[:, 0:2, :]))
                nc.vector.tensor_copy(brows[32 * a:32 * a + 1, :, :, :],
                                      part[32 * a:32 * a + 1, :, :].unsqueeze(2).to_broadcast((1, 2, 4, F)))
                if a < 2:
                    chained(nc.vector.tensor_tensor(out=rest[:, :, :], in0=value[:, 0:2, :], in1=part[:, :, :],
                                                    op=ALU.subtract))
                value = rest
            chained(nc.vector.memset(bias[:, 0:1], 0.0))
            for l in range(NRES):
                for half, raw in ((0, l), (1, NRES + l)):
                    c = 2 * l + half
                    nc.vector.tensor_scalar(less[:, c:c + 1], bias[:, c:c + 1], -LN2, None, ALU.add).then_inc(s_less, 1)
                    dve.wait_ge(s_bps, 2 + c)
                    if half == 0:
                        chained(nc.vector.tensor_tensor(out=bias[:, c + 1:c + 2], in0=ps[:, 7, c:c + 1],
                                                        in1=braw[:, raw:raw + 1], op=ALU.add))
                    else:
                        chained(nc.vector.scalar_tensor_tensor(out=bias[:, c + 1:c + 2], in0=ps[:, 7, c:c + 1],
                                                               scalar=braw[:, raw:raw + 1], in1=bias[:, c - 1:c],
                                                               op0=ALU.add, op1=ALU.add))
            c = 2 * NRES
            chained(nc.vector.tensor_reduce(out=amax[:, :], in_=bias[:, :], axis=mybir.AxisListType.X, op=ALU.max,
                                            apply_absolute_value=True))
            nc.vector.tensor_scalar(dmat[:, :], negln2[:, :], bias[:, c:c + 1], None, ALU.add).then_inc(s_less, 1)
            dve.wait_ge(s_bps, 2 + c)
            chained(nc.vector.tensor_tensor(out=brow[:, 2, :], in0=ps[:, 7, 256:384], in1=brow[:, 2, :], op=ALU.add))
            chained(nc.vector.tensor_reduce(out=gmax[:, :], in_=ps[0:1, 7, 384:512], axis=mybir.AxisListType.X,
                                            op=ALU.max))
            nc.vector.tensor_scalar(flag[:, :], gmax[:, :], LIMIT, None, ALU.is_gt).then_inc(s_bias, 1)

            def step(k, p, front, mid, back):
                g = 2 * k + p
                for u in range(UNITS):
                    if (front or u < 2 and mid) and not (isinstance(g, int) and g == 0 and u < 2):
                        v = UNITS * g + u - 2
                        b, q = u % 2, 1 - u // 2
                        dve.wait_ge(s_PL, v + 1)
                        before = g if q == 0 else g - 1
                        if not (isinstance(before, int) and before == 0):
                            dve.wait_ge(s_sp[q], 16 * before)
                        nc.vector.scalar_tensor_tensor(
                            out=z[:, q, 4 * b:4 * b + 4, :].rearrange("p j f -> p (j f)"),
                            in0=t[:, 1, b * HALF:(b + 1) * HALF], scalar=CAP,
                            in1=ps[:, 6 + b, :], op0=ALU.min, op1=ALU.max).then_inc(s_PU, 1)
                    if front:
                        v = UNITS * g + u
                        dve.wait_ge(s_XL, v + 1)
                        if not (isinstance(g, int) and g == 0 and u < 2):
                            dve.wait_ge(s_P, v - 1)
                        b = u % 2
                        nc.vector.scalar_tensor_tensor(out=ug[:, 0, b * HALF:(b + 1) * HALF],
                                                       in0=t[:, 0, b * HALF:(b + 1) * HALF], scalar=CAP,
                                                       in1=ps[:, 4 + b, :], op0=ALU.min,
                                                       op1=ALU.max).then_inc(s_XU, 1)
                    if front and u == 2:
                        dve.wait_ge(s_ln, g + 1)
                        if not (isinstance(g, int) and g < 2):
                            dve.wait_ge(s_J, g - 1)
                        nc.vector.scalar_tensor_tensor(out=xaT[:, p, :], in0=te[:, 0, :], scalar=CAP,
                                                       in1=ps[:, p, :], op0=ALU.min, op1=ALU.max).then_inc(s_xa, 1)
                    if mid:
                        m, pm = g - 1, (p + 1) % 2
                        km = (m - pm) // 2 if isinstance(m, int) else (k if pm == 0 else k - 1)
                        if u == 0:
                            dve.wait_ge(s_aT, m + 1)
                            if not (isinstance(m, int) and m == 0):
                                dve.wait_ge(s_G, m)
                            nc.vector.tensor_copy(attrT[:, :], ps[:, 2, 0:EG // 2]).then_inc(s_aTs, 1)
                            tail = 16 if isinstance(m, int) and m == EGROUPS - 1 else 0
                            dve.wait_ge(s_la[pm], 32 * (km + 1) + tail)
                        targets = srow_tail[:, :] if isinstance(m, int) and m == EGROUPS - 1 else srow[:, pm, :]
                        for j in ((3,), (2, 1), (0,), ())[u]:
                            last = nc.vector.scalar_tensor_tensor(
                                out=same[:, pm, j, 0:(j + 1) * 128], in0=targets[:, 0:(j + 1) * 128],
                                scalar=src_f[:, bass.ds(4 * m + j, 1)], in1=mask[:, (ET - 1 - j) * 128:EG],
                                op0=ALU.is_equal, op1=ALU.mult, accum_out=cnt[:, pm, j:j + 1])
                        if u == 2:
                            last.then_inc(s_same, 1)
                    if back and u == 2:
                        c = g - 2
                        dve.wait_ge(s_D, c + 1)
                        nc.vector.tensor_copy(comb[:, p, :], ps[:, 3, :]).then_inc(s_comb, 1)
                    if mid and u == 2:
                        dve.wait_ge(s_same, m + 1)
                        nc.vector.scalar_tensor_tensor(out=sel[:, :], in0=cnt[:, pm, :], scalar=1.0,
                                                       in1=diff_f[:, bass.ds(4 * m, ET)],
                                                       op0=ALU.is_equal, op1=ALU.mult).then_inc(s_sel, 1)
                    if mid and u == 3:
                        dve.wait_ge(s_sel, m + 1)
                        if not (isinstance(m, int) and m < 2):
                            dve.wait_ge(s_sc, 16 * ET * (m - 1))
                        nc.vector.tensor_tensor(out=rows[:, pm, :], in0=sel[:, :], in1=dump_f[:, :],
                                                op=ALU.add).then_inc(s_rows, 1)
                        dve.wait_ge(s_ln2, m + 1)
                        nc.vector.scalar_tensor_tensor(out=xjf[:, :], in0=te[:, 1, :], scalar=CAP,
                                                       in1=ps[:, pm, :], op0=ALU.min,
                                                       op1=ALU.max).then_inc(s_xjf, 1)
                        dve.wait_ge(s_xjf, m + 1)
                        dve.wait_ge(s_G, m + 1)
                        nc.vector.scalar_tensor_tensor(out=pxj[:, pm, :], in0=xjf[:, :], scalar=-LN2,
                                                       in1=ps[:, 2, :], op0=ALU.add,
                                                       op1=ALU.mult).then_inc(s_px, 1)

            edges(dve, step)
            dve.wait_ge(s_bias, 1)

            def softplus(i, s, q, short):
                n = PER * i + 2 * (s - 2) + q
                lo = bank(s, q)
                target = uf if s == STEPS - 1 else ug
                if s == STEPS - 1 and not (isinstance(i, int) and i == 0):
                    dve.wait_ge(s_o, 2 * (2 * (i - 1) + q) + 2)
                if short or s == 2:
                    for h in range(2):
                        before = s == 2 and not (isinstance(i, int) and i == 0)
                        if before and (h == 0 or q == 0):
                            add_x(i - 1, q, h)
                        dve.wait_ge(s_log, 2 * n + h + 1)
                        half = slice(h * HALF, (h + 1) * HALF)
                        nc.vector.scalar_tensor_tensor(out=target[:, q, half], in0=t[:, q, half], scalar=CAP,
                                                       in1=ps[:, lo + h, :], op0=ALU.min,
                                                       op1=ALU.max).then_inc(s_u, 1)
                        if before and h == 1 and q == 1:
                            add_x(i - 1, q, h)
                    return
                nm = (PER - 2) * i + 2 * (s - 3) + q
                for h in range(2):
                    dve.wait_ge(s_log, 2 * n + h + 1)
                    half = slice(h * HALF, (h + 1) * HALF)
                    nc.vector.tensor_scalar(t[:, q, half], t[:, q, half], CAP, bias[:, s - 2:s - 1], ALU.min,
                                            ALU.subtract).then_inc(s_min, 1)
                for h in range(2):
                    half = slice(h * HALF, (h + 1) * HALF)
                    dve.wait_ge(s_min, 2 * nm + h + 1)
                    nc.vector.tensor_tensor(out=target[:, q, half], in0=ps[:, lo + h, :], in1=t[:, q, half],
                                            op=ALU.max).then_inc(s_u, 1)

            def add_x(i, q, h):
                n = 2 * i + q
                dve.wait_ge(s_xu, n + 1)
                if not (isinstance(i, int) and i == 0):
                    dve.wait_ge(s_out[q], 16 * i)
                dve.wait_ge(s_o, 2 * n + h + 1)
                nc.vector.tensor_tensor(out=z[:, q, 4 * h:4 * h + 4, :],
                                        in0=ps[:, 4 * q + 2 + h, :].rearrange("p (j f) -> p j f", f=F),
                                        in1=x_nat[:, q, 4 * h:4 * h + 4, :], op=ALU.add).then_inc(s_z, 1)

            def row_stats(i, q, h):
                n = 2 * i + q
                dve.wait_ge(s_z, 2 * n + h + 1)
                for j in range(4 * h, 4 * h + 4):
                    last = nc.vector.bn_stats(stats[:, q, j, :], z[:, q, j, :])
                if h:
                    last.then_inc(s_st, 1)

            def mean_variance(i, q):
                n = 2 * i + q
                dve.wait_ge(s_st, n + 1)
                dve.sem_inc(s_dpass, 1)
                for j in range(TILES):
                    last = nc.vector.bn_aggr(mv[:, q, j, :], stats[:, q, j, :])
                last.then_inc(s_mv, 1)

            def pair(i, short, first=False):
                for s in range(2, STEPS):
                    for q in range(2):
                        softplus(i, s, q, short)
                        if first:
                            continue
                        if s == 3:
                            row_stats(i - 1, 0, q)
                        if (s, q) == (4, 0):
                            mean_variance(i - 1, 0)
                        if (s, q) == (4, 1):
                            row_stats(i - 1, 1, 0)
                        if (s, q) == (5, 0):
                            row_stats(i - 1, 1, 1)
                        if (s, q) == (5, 1):
                            mean_variance(i - 1, 1)

            def all_pairs(short):
                pair(0, short, first=True)
                with dve.Fori(1, PAIRS) as i:
                    pair(i, short)

            large = dve.value_load(flag[0:1, 0:1], min_val=0, max_val=1)
            with dve.If(large == 0):
                all_pairs(short=True)
            with dve.Else():
                all_pairs(short=False)
            for q in range(2):
                for h in range(2):
                    add_x(PAIRS - 1, q, h)
            for q in range(2):
                row_stats(PAIRS - 1, q, 0)
                row_stats(PAIRS - 1, q, 1)
                mean_variance(PAIRS - 1, q)

        @block.tensor
        def _(pe):
            pe.wait_ge(s_const, 3)
            pe.wait_ge(s_cdve, 1)
            for c in range(2):
                for h in range(2):
                    last = nc.tensor.transpose(ps[:, c, h * 128:(h + 1) * 128], irow_f[:, c, h, :], ident[:, :])
            last.then_inc(s_iT, 1)
            pe.wait_ge(s_w, NW)
            nc.tensor.matmul(ps[:, 7, 128:256], negln2[:, :], wi[:, :], start=True, stop=True)
            nc.tensor.matmul(ps[:, 7, 384:512], negln2[:, :], wj[:, :], start=True, stop=True).then_inc(s_bps, 1)
            for c in range(2 * NRES):
                pe.wait_ge(s_less, c + 1)
                w = w2[:, c // 2, :] if c % 2 else w1[:, c // 2, :]
                nc.tensor.matmul(ps[:, 7, c:c + 1], w, less[:, c:c + 1], start=True, stop=True).then_inc(s_bps, 1)
            pe.wait_ge(s_less, 1 + 2 * NRES)
            nc.tensor.matmul(ps[:, 7, 256:384], dmat[:, :], wo[:, :], start=True, stop=True)
            nc.tensor.matmul(ps[0:1, 7, 384:512], amax[:, :], ident[:, :], start=True, stop=True).then_inc(s_bps, 1)
            pe.wait_ge(s_bias, 1)

            def biased(o, row, tiles, w):
                nc.tensor.matmul(o, ones[:, :], brows[:, row, :, :].rearrange("p j f -> p (j f)"), start=True,
                                 stop=False, skip_group_check=True)
                for j in range(4):
                    last = nc.tensor.matmul(o[:, j * F:(j + 1) * F], tiles[:, j * 128:(j + 1) * 128], w,
                                            start=False, stop=True, skip_group_check=True)
                return last

            def atoms0(g, u):
                v, b = UNITS * g + u, u % 2
                if b == 0:
                    pe.wait_ge(s_x[u // 2], 16 * (g + 1))
                if not (isinstance(g, int) and g == 0 and u < 2):
                    pe.wait_ge(s_XU, v - 1)
                for j in range(4):
                    last = nc.tensor.transpose(ps[:, 4 + b, j * 128:(j + 1) * 128],
                                               x_nat[:, u // 2, 4 * b + j, :], ident[:, :])
                last.then_inc(s_X, 1)

            def atoms1(g, u):
                v, b = UNITS * g + u - 1, (u + 1) % 2
                pe.wait_ge(s_XU, v + 1)
                if not (isinstance(v, int) and v < 2):
                    pe.wait_ge(s_PU, v - 1)
                biased(ps[:, 6 + b, :], 0, ug[:, 0, b * HALF:(b + 1) * HALF], wi[:, :]).then_inc(s_P, 1)

            def step(k, p, front, mid, back):
                g = 2 * k + p
                m, pm = g - 1, (p + 1) % 2
                for u in range(UNITS):
                    if front and u < UNITS - 1:
                        atoms0(g, u + 1)
                    elif front and not (isinstance(g, int) and g == PAIRS - 1):
                        atoms0(g + 1, 0)
                    if (front or u == 0 and mid) and not (isinstance(g, int) and g == 0 and u == 0):
                        atoms1(g, u)
                    if front and u == 0:
                        pe.wait_ge(s_ga[p], 16 * ET * (k + 1))
                        if not (isinstance(g, int) and g < 2):
                            pe.wait_ge(s_xjf, g - 1)
                        for j in range(ET):
                            last = nc.tensor.transpose(ps[:, p, j * 128:(j + 1) * 128], xe[:, p, j, :], ident[:, :])
                        last.then_inc(s_xT, 1)
                    if mid and u == 0:
                        km = (m - pm) // 2 if isinstance(m, int) else (k if pm == 0 else k - 1)
                        tail = 16 if isinstance(m, int) and m == EGROUPS - 1 else 0
                        pe.wait_ge(s_la[pm], 32 * (km + 1) + tail)
                        if not (isinstance(m, int) and m == 0):
                            pe.wait_ge(s_px, m)
                        for j in range(ET // 2):
                            last = nc.tensor.transpose(ps[:, 2, j * 128:(j + 1) * 128],
                                                       attr[:, pm, 2 * j:2 * j + 2, :].rearrange("p j c -> p (j c)"),
                                                       ident[:, :])
                        last.then_inc(s_aT, 1)
                    if mid and u == 1:
                        pe.wait_ge(s_aTs, m + 1)
                        for j in range(ET // 2):
                            last = nc.tensor.matmul(ps[:, 2, 2 * j * F:(2 * j + 2) * F],
                                                    attrT[:, j * 128:(j + 1) * 128],
                                                    wk[:, :, :].rearrange("k j f -> k (j f)"), start=True, stop=True)
                        last.then_inc(s_G, 1)
                    if back and u < 3:
                        c = g - 2
                        if u == 0:
                            pe.wait_ge(s_px, c + 1)
                            pe.wait_ge(s_same, c + 1)
                            if not (isinstance(c, int) and c == 0):
                                pe.wait_ge(s_comb, c)
                        for j in ((0,), (1,), range(2, ET))[u]:
                            for jj in range(j, ET):
                                last = nc.tensor.matmul(ps[:, 3, j * F:(j + 1) * F],
                                                        same[:, p, jj, j * 128:(j + 1) * 128],
                                                        pxj[:, p, jj * F:(jj + 1) * F],
                                                        start=(jj == j), stop=(jj == ET - 1))
                        if u == 2:
                            last.then_inc(s_D, 1)
                    if front and u == 3:
                        pe.wait_ge(s_xa, g + 1)
                        biased(ps[:, p, :], 1, xaT[:, p, :], wj[:, :]).then_inc(s_J, 1)

            atoms0(0, 0)
            edges(pe, step)
            pe.wait_ge(s_comb, EGROUPS)
            pe.wait_ge(s_PU, UNITS * PAIRS)

            def layer(i, s, q):
                n = PER * i + 2 * (s - 2) + q
                lo = bank(s, q)
                if s == 2:
                    pe.wait_ge(s_add, 2 * i + q + 1)
                    for h in range(2):
                        if not (isinstance(i, int) and i == 0):
                            pe.wait_ge(s_u, 2 * (n - 2) + h + 1)
                        for j in range(4):
                            last = nc.tensor.matmul(ps[:, lo + h, j * 128:(j + 1) * 128],
                                                    xj_nat[:, q, 4 * h + j, :], ident[:, :], is_transpose=True,
                                                    start=(j == 0), stop=True, skip_group_check=True)
                        last.then_inc(s_pe, 1)
                    return
                w = w1[:, (s - 3) // 2, :] if s % 2 else w2[:, (s - 4) // 2, :]
                for h in range(2):
                    if s == 3 and not (isinstance(i, int) and i == 0):
                        pe.wait_ge(s_z, 2 * (2 * (i - 1) + q) + h + 1)
                    pe.wait_ge(s_u, 2 * (n - 2) + h + 1)
                    nc.tensor.matmul(ps[:, lo + h, :], w, ug[:, q, h * HALF:(h + 1) * HALF],
                                     start=bool(s % 2), stop=True,
                                     skip_group_check=not s % 2).then_inc(s_pe, 1)

            def output(i, q, h):
                n = PER * i + 2 * (STEPS - 3) + q
                pe.wait_ge(s_u, 2 * n + h + 1)
                for j in range(4):
                    c = 4 * h + j
                    last = nc.tensor.matmul(ps[:, 4 * q + 2 + h, j * F:(j + 1) * F], uf[:, q, c * 128:(c + 1) * 128],
                                            wo[:, :], start=True, stop=True)
                last.then_inc(s_o, 1)

            def pair(i):
                layer(i, 2, 0)
                output(i - 1, 0, 0)
                output(i - 1, 0, 1)
                layer(i, 2, 1)
                output(i - 1, 1, 0)
                layer(i, 3, 0)
                output(i - 1, 1, 1)
                layer(i, 3, 1)
                for s in range(4, STEPS):
                    for q in range(2):
                        layer(i, s, q)

            for s in range(2, STEPS):
                for q in range(2):
                    layer(0, s, q)
            with pe.Fori(1, PAIRS) as i:
                pair(i)
            for q in range(2):
                for h in range(2):
                    output(PAIRS - 1, q, h)


_INS = ['x', 'src', 'dst', 'edge_attr_64', 'L0_gnn_W_k2f', 'L0_gnn_W_i', 'L0_gnn_b_i', 'L0_gnn_W_j', 'L0_gnn_b_j',
        'L0_gnn_W_res1', 'L0_gnn_b_res1', 'L0_gnn_W_res2', 'L0_gnn_b_res2', 'L0_gnn_W_out', 'L0_gnn_b_out',
        'L0_gnn_u']


def kernel(**inputs):
    import numpy as _np
    import concourse.bacc as _bacc
    from concourse import mybir as _mybir
    from concourse.bass_utils import run_bass_kernel_spmd as _run

    nc = _bacc.Bacc("TRN2", target_bir_lowering=False, num_devices=1)
    arrays, args = {}, []
    for name in _INS:
        a = _np.ascontiguousarray(inputs[name])
        arrays[f"in_{name}_dram"] = a
        args.append(nc.dram_tensor(f"in_{name}_dram", a.shape, _mybir.dt.from_np(a.dtype), kind="ExternalInput").ap())
    shape = inputs['x'].shape
    args.append(nc.dram_tensor("out_0_dram", shape, _mybir.dt.float32, kind="ExternalOutput").ap())
    gnn_kernel(nc, *args)
    r = _run(nc, [arrays], core_ids=[0])
    return r.results[0]["out_0_dram"]
```
